# Optimizing a Trainium2 kernel written in Bass

```python
import numpy as np
import jax
import jax.numpy as jnp

def _softmax(x, axis=-1):
    return jax.nn.softmax(x, axis=axis)

def _gelu(x):
    return jax.nn.gelu(x, approximate=True)

def _silu(x):
    return jax.nn.silu(x)

def _sigmoid(x):
    return jax.nn.sigmoid(x)

def _layernorm(x, axis=-1, eps=1e-05):
    m = jnp.mean(x, axis=axis, keepdims=True)
    v = jnp.var(x, axis=axis, keepdims=True)
    return (x - m) / jnp.sqrt(v + eps)

def _scatter_add(tgt, idx, src, axis=0):
    return tgt.at[idx].add(src)

def _segment_sum(src, seg, n):
    return jax.ops.segment_sum(src, seg, n)
kernel_name = 'mk_dlrm_tower_d1_rec_r8_a6b819'

def setup_inputs(seed: int=0):
    np.random.seed(seed)
    _w = jnp.asarray

    def _rec_inputs():
        import jax
        import jax.numpy as jnp
        _tk = jax.random.key(seed)
        dense_ctx = jax.random.normal(jax.random.fold_in(_tk, 190), (1024, 16), jnp.float32)
        ids = jnp.stack([jax.random.randint(jax.random.fold_in(_tk, 200 + f), (1024,), 0, v, jnp.int32) for f, v in enumerate([1000, 12500, 1000, 1000, 12500, 1000, 12500, 12500, 12500, 12500, 1250, 1000, 125000, 1250, 125000, 1000, 125000, 1250, 1250, 1000, 1250, 1250, 1250, 12500, 1250, 1250, 125000, 125000, 1000, 1000, 1000, 12500])], axis=1)
        tbl_0 = 0.05 * jax.random.normal(jax.random.fold_in(_tk, 500 + 0), (1000, 32), jnp.float32)
        tbl_1 = 0.05 * jax.random.normal(jax.random.fold_in(_tk, 500 + 1), (12500, 32), jnp.float32)
        tbl_2 = 0.05 * jax.random.normal(jax.random.fold_in(_tk, 500 + 2), (1000, 32), jnp.float32)
        tbl_3 = 0.05 * jax.random.normal(jax.random.fold_in(_tk, 500 + 3), (1000, 32), jnp.float32)
        tbl_4 = 0.05 * jax.random.normal(jax.random.fold_in(_tk, 500 + 4), (12500, 32), jnp.float32)
        tbl_5 = 0.05 * jax.random.normal(jax.random.fold_in(_tk, 500 + 5), (1000, 32), jnp.float32)
        tbl_6 = 0.05 * jax.random.normal(jax.random.fold_in(_tk, 500 + 6), (12500, 32), jnp.float32)
        tbl_7 = 0.05 * jax.random.normal(jax.random.fold_in(_tk, 500 + 7), (12500, 32), jnp.float32)
        tbl_8 = 0.05 * jax.random.normal(jax.random.fold_in(_tk, 500 + 8), (12500, 32), jnp.float32)
        tbl_9 = 0.05 * jax.random.normal(jax.random.fold_in(_tk, 500 + 9), (12500, 32), jnp.float32)
        tbl_10 = 0.05 * jax.random.normal(jax.random.fold_in(_tk, 500 + 10), (1250, 32), jnp.float32)
        tbl_11 = 0.05 * jax.random.normal(jax.random.fold_in(_tk, 500 + 11), (1000, 32), jnp.float32)
        tbl_12 = 0.05 * jax.random.normal(jax.random.fold_in(_tk, 500 + 12), (125000, 32), jnp.float32)
        tbl_13 = 0.05 * jax.random.normal(jax.random.fold_in(_tk, 500 + 13), (1250, 32), jnp.float32)
        tbl_14 = 0.05 * jax.random.normal(jax.random.fold_in(_tk, 500 + 14), (125000, 32), jnp.float32)
        tbl_15 = 0.05 * jax.random.normal(jax.random.fold_in(_tk, 500 + 15), (1000, 32), jnp.float32)
        tbl_16 = 0.05 * jax.random.normal(jax.random.fold_in(_tk, 500 + 16), (125000, 32), jnp.float32)
        tbl_17 = 0.05 * jax.random.normal(jax.random.fold_in(_tk, 500 + 17), (1250, 32), jnp.float32)
        tbl_18 = 0.05 * jax.random.normal(jax.random.fold_in(_tk, 500 + 18), (1250, 32), jnp.float32)
        tbl_19 = 0.05 * jax.random.normal(jax.random.fold_in(_tk, 500 + 19), (1000, 32), jnp.float32)
        tbl_20 = 0.05 * jax.random.normal(jax.random.fold_in(_tk, 500 + 20), (1250, 32), jnp.float32)
        tbl_21 = 0.05 * jax.random.normal(jax.random.fold_in(_tk, 500 + 21), (1250, 32), jnp.float32)
        tbl_22 = 0.05 * jax.random.normal(jax.random.fold_in(_tk, 500 + 22), (1250, 32), jnp.float32)
        tbl_23 = 0.05 * jax.random.normal(jax.random.fold_in(_tk, 500 + 23), (12500, 32), jnp.float32)
        tbl_24 = 0.05 * jax.random.normal(jax.random.fold_in(_tk, 500 + 24), (1250, 32), jnp.float32)
        tbl_25 = 0.05 * jax.random.normal(jax.random.fold_in(_tk, 500 + 25), (1250, 32), jnp.float32)
        tbl_26 = 0.05 * jax.random.normal(jax.random.fold_in(_tk, 500 + 26), (125000, 32), jnp.float32)
        tbl_27 = 0.05 * jax.random.normal(jax.random.fold_in(_tk, 500 + 27), (125000, 32), jnp.float32)
        tbl_28 = 0.05 * jax.random.normal(jax.random.fold_in(_tk, 500 + 28), (1000, 32), jnp.float32)
        tbl_29 = 0.05 * jax.random.normal(jax.random.fold_in(_tk, 500 + 29), (1000, 32), jnp.float32)
        tbl_30 = 0.05 * jax.random.normal(jax.random.fold_in(_tk, 500 + 30), (1000, 32), jnp.float32)
        tbl_31 = 0.05 * jax.random.normal(jax.random.fold_in(_tk, 500 + 31), (12500, 32), jnp.float32)
        _rk = jax.random.fold_in(_tk, 7)
        W_top1 = 0.0606339 * jax.random.normal(jax.random.fold_in(_tk, 801), (272, 512), jnp.float32)
        W_top2 = 0.0441942 * jax.random.normal(jax.random.fold_in(_tk, 802), (512, 256), jnp.float32)
        W_top3 = 0.0625 * jax.random.normal(jax.random.fold_in(_tk, 803), (256, 1), jnp.float32)
        b_top1 = jnp.zeros((512,), jnp.float32)
        b_top2 = jnp.zeros((256,), jnp.float32)
        return (dense_ctx, ids, tbl_0, tbl_1, tbl_2, tbl_3, tbl_4, tbl_5, tbl_6, tbl_7, tbl_8, tbl_9, tbl_10, tbl_11, tbl_12, tbl_13, tbl_14, tbl_15, tbl_16, tbl_17, tbl_18, tbl_19, tbl_20, tbl_21, tbl_22, tbl_23, tbl_24, tbl_25, tbl_26, tbl_27, tbl_28, tbl_29, tbl_30, tbl_31, W_top1, b_top1, W_top2, b_top2, W_top3)
    dense_ctx, ids, tbl_0, tbl_1, tbl_2, tbl_3, tbl_4, tbl_5, tbl_6, tbl_7, tbl_8, tbl_9, tbl_10, tbl_11, tbl_12, tbl_13, tbl_14, tbl_15, tbl_16, tbl_17, tbl_18, tbl_19, tbl_20, tbl_21, tbl_22, tbl_23, tbl_24, tbl_25, tbl_26, tbl_27, tbl_28, tbl_29, tbl_30, tbl_31, W_top1, b_top1, W_top2, b_top2, W_top3 = _rec_inputs()

    def _L0_rec_setup():
        import jax, jax.numpy as jnp
        import numpy as np
        B, F, D = (512, 32, 32)
        LAYER_SIZE = [128, 128]

        def _cin_forward(inputs, filters):
            x0 = inputs
            prev = inputs
            outs = []
            for W in filters:
                z = jnp.einsum('bhd,bmd->bhmd', x0, prev)
                b, h, m, d = z.shape
                z = z.reshape(b, h * m, d)
                cur = jnp.einsum('bpd,pn->bnd', z, W[0])
                cur = jax.nn.relu(cur)
                prev = cur
                outs.append(cur)
            result = jnp.concatenate(outs, axis=1)
            return jnp.sum(result, axis=-1)
        key = jax.random.key(seed)
        k1, k2, k3 = jax.random.split(key, 3)
        inputs = jax.random.normal(k1, (B, F, D), dtype=jnp.float32)
        field_nums = [F] + LAYER_SIZE
        filter_0 = jax.random.normal(k2, (1, field_nums[0] * field_nums[0], field_nums[1]), dtype=jnp.float32) * 0.05
        filter_1 = jax.random.normal(k3, (1, field_nums[0] * field_nums[1], field_nums[2]), dtype=jnp.float32) * 0.05
        return {'inputs': inputs, 'filter_0': filter_0, 'filter_1': filter_1}
    _L0_rec_all = _L0_rec_setup()
    _L0_rec_in = {k: v for k, v in _L0_rec_all.items() if k in ('filter_0', 'filter_1')}
    del _L0_rec_all
    return {'dense_ctx': dense_ctx, 'ids': ids, 'tbl_0': tbl_0, 'tbl_1': tbl_1, 'tbl_2': tbl_2, 'tbl_3': tbl_3, 'tbl_4': tbl_4, 'tbl_5': tbl_5, 'tbl_6': tbl_6, 'tbl_7': tbl_7, 'tbl_8': tbl_8, 'tbl_9': tbl_9, 'tbl_10': tbl_10, 'tbl_11': tbl_11, 'tbl_12': tbl_12, 'tbl_13': tbl_13, 'tbl_14': tbl_14, 'tbl_15': tbl_15, 'tbl_16': tbl_16, 'tbl_17': tbl_17, 'tbl_18': tbl_18, 'tbl_19': tbl_19, 'tbl_20': tbl_20, 'tbl_21': tbl_21, 'tbl_22': tbl_22, 'tbl_23': tbl_23, 'tbl_24': tbl_24, 'tbl_25': tbl_25, 'tbl_26': tbl_26, 'tbl_27': tbl_27, 'tbl_28': tbl_28, 'tbl_29': tbl_29, 'tbl_30': tbl_30, 'tbl_31': tbl_31, 'W_top1': W_top1, 'b_top1': b_top1, 'W_top2': W_top2, 'b_top2': b_top2, 'W_top3': W_top3, 'L0_rec_filter_0': _L0_rec_in['filter_0'], 'L0_rec_filter_1': _L0_rec_in['filter_1']}

def reference(dense_ctx, ids, tbl_0, tbl_1, tbl_2, tbl_3, tbl_4, tbl_5, tbl_6, tbl_7, tbl_8, tbl_9, tbl_10, tbl_11, tbl_12, tbl_13, tbl_14, tbl_15, tbl_16, tbl_17, tbl_18, tbl_19, tbl_20, tbl_21, tbl_22, tbl_23, tbl_24, tbl_25, tbl_26, tbl_27, tbl_28, tbl_29, tbl_30, tbl_31, W_top1, b_top1, W_top2, b_top2, W_top3, L0_rec_filter_0, L0_rec_filter_1):
    import jax
    import jax.numpy as jnp

    def _L0_rec_ref(inputs, filter_0, filter_1):
        import jax, jax.numpy as jnp
        import numpy as np
        B, F, D = (512, 32, 32)
        LAYER_SIZE = [128, 128]

        def _cin_forward(inputs, filters):
            x0 = inputs
            prev = inputs
            outs = []
            for W in filters:
                z = jnp.einsum('bhd,bmd->bhmd', x0, prev)
                b, h, m, d = z.shape
                z = z.reshape(b, h * m, d)
                cur = jnp.einsum('bpd,pn->bnd', z, W[0])
                cur = jax.nn.relu(cur)
                prev = cur
                outs.append(cur)
            result = jnp.concatenate(outs, axis=1)
            return jnp.sum(result, axis=-1)
        return _cin_forward(inputs, (filter_0, filter_1))
    e = jnp.stack([tbl_0[ids[:, 0]], tbl_1[ids[:, 1]], tbl_2[ids[:, 2]], tbl_3[ids[:, 3]], tbl_4[ids[:, 4]], tbl_5[ids[:, 5]], tbl_6[ids[:, 6]], tbl_7[ids[:, 7]], tbl_8[ids[:, 8]], tbl_9[ids[:, 9]], tbl_10[ids[:, 10]], tbl_11[ids[:, 11]], tbl_12[ids[:, 12]], tbl_13[ids[:, 13]], tbl_14[ids[:, 14]], tbl_15[ids[:, 15]], tbl_16[ids[:, 16]], tbl_17[ids[:, 17]], tbl_18[ids[:, 18]], tbl_19[ids[:, 19]], tbl_20[ids[:, 20]], tbl_21[ids[:, 21]], tbl_22[ids[:, 22]], tbl_23[ids[:, 23]], tbl_24[ids[:, 24]], tbl_25[ids[:, 25]], tbl_26[ids[:, 26]], tbl_27[ids[:, 27]], tbl_28[ids[:, 28]], tbl_29[ids[:, 29]], tbl_30[ids[:, 30]], tbl_31[ids[:, 31]]], axis=1)
    z = _L0_rec_ref(e, L0_rec_filter_0, L0_rec_filter_1)
    z = z.reshape(z.shape[0], -1)
    h = jnp.concatenate([z, dense_ctx], axis=1)
    h = jnp.maximum(h @ W_top1 + b_top1, 0.0)
    h = jnp.maximum(h @ W_top2 + b_top2, 0.0)
    y = h @ W_top3
    return y

_drawn_inputs = setup_inputs


def setup_inputs(seed=0):
    import zlib

    import numpy as np

    out = dict(_drawn_inputs(seed))
    spreads = {'b_top1': (0.0, 0.439), 'b_top2': (0.0, 0.428)}
    factors = {'tbl_0': 6.012,
     'tbl_1': 5.937,
     'tbl_2': 6.073,
     'tbl_3': 6.03,
     'tbl_4': 5.903,
     'tbl_5': 5.967,
     'tbl_6': 6.035,
     'tbl_7': 6.317,
     'tbl_8': 6.18,
     'tbl_9': 5.945,
     'tbl_10': 5.738,
     'tbl_11': 6.032,
     'tbl_12': 5.999,
     'tbl_13': 6.175,
     'tbl_14': 6.19,
     'tbl_15': 6.01,
     'tbl_16': 6.393,
     'tbl_17': 5.781,
     'tbl_18': 6.319,
     'tbl_19': 6.456,
     'tbl_20': 5.966,
     'tbl_21': 6.065,
     'tbl_22': 6.289,
     'tbl_23': 5.833,
     'tbl_24': 6.158,
     'tbl_25': 6.051,
     'tbl_26': 5.86,
     'tbl_27': 6.238,
     'tbl_28': 6.211,
     'tbl_29': 6.238,
     'tbl_30': 5.98,
     'tbl_31': 5.795,
     'L0_rec_filter_1': 8.0}
    for name, (base, spread) in spreads.items():
        noise = np.random.default_rng([zlib.crc32(name.encode()), seed]).standard_normal(out[name].shape)
        drawn = base * np.exp(spread * noise) if base else spread * noise
        out[name] = jnp.asarray(drawn.astype(out[name].dtype))
    for name, factor in factors.items():
        out[name] = (out[name] * factor).astype(out[name].dtype)
    return out
```

```python
import concourse.bass as bass
from concourse import mybir
from contextlib import ExitStack

F32 = mybir.dt.float32
F32R = mybir.dt.float32r
I32 = mybir.dt.int32
ALU = mybir.AluOpType
ACT = mybir.ActivationFunctionType

B, F, D = 1024, 32, 32
N = 128
P = 128
BT = B // P
DG = 4
TPB = D // DG
T = BT * TPB
C = DG * P
CHUNKS = 4
HG = C // N
GROUPS = F // HG
HALF = GROUPS // 2
D_BANKS, A_BANKS = 4, 2
D_OPS = DG * HALF * HG
A_GROUPS = DG * HALF
Z_OPS = CHUNKS + 1
POOL_OPS = 3 * DG + 3
COMBINE_OPS = 3
H1, H2, DENSE = 512, 256, 16
HALF_B = 512


def build_cin_tower(nc, dense_t, ids, tables, w0_pairs, w0_swapped, w0_last, w1, wt1, bt1, wt2, bt2, wt3, out):
    ctx = ExitStack()
    with ctx:
        def sb(name, shape, dt=F32):
            return ctx.enter_context(nc.sbuf_tensor(name, shape, dt))

        def sem(name):
            return ctx.enter_context(nc.semaphore(name))

        x_rows = nc.dram_tensor("x_rows", (F + F // 2, T * C), F32, kind="Internal").ap()

        w1h = sb("w1h", [P, F, N], F32R)
        w1l = sb("w1l", [P, F, N], F32R)
        w0 = sb("w0", [P, CHUNKS, N])
        w0b = sb("w0b", [P, CHUNKS, N])
        w0c = sb("w0c", [F, N])
        ident = sb("ident", [P, P])
        ids_all = sb("ids_all", [P, BT, F], I32)
        ids_now = sb("ids_now", [P, F], I32)
        landing = sb("landing", [P, F, D])
        e_ring = sb("e_ring", [P, 2 * TPB, C // DG])
        x_t = sb("x_t", [P, F // 4, P])
        xb = sb("xb", [P, 2, CHUNKS + 1, C])
        xb_last = sb("xb_last", [F, 2, C])
        z = sb("z", [P, 2, CHUNKS, C])
        z_last = sb("z_last", [F, 2, C])
        p_full = sb("p_full", [P, 2, C])
        p_hi = sb("p_hi", [P, 2, C], F32R)
        p_lo = sb("p_lo", [P, 2, C], F32R)
        x_now = sb("x_now", [P, 2, DG, F])
        scaled = sb("scaled", [P, 2 * HALF, HG * N])
        pair = sb("pair", [P, 2, HG * N])
        a_sum = sb("a_sum", [P, DG, HG * N])
        a_fold = sb("a_fold", [P, DG, 2 * N])
        a_part = sb("a_part", [P, 2, DG, N])
        d_part = sb("d_part", [P, 2, DG, 2, N])
        d_fold = sb("d_fold", [P, DG, N])
        cur = sb("cur", [P, DG, N])
        sum1 = sb("sum1", [P, BT, C])
        sum2 = sb("sum2", [P, BT, DG, N])
        wt1_sb = sb("wt1_sb", [P, 2, H1])
        wt1_dense = sb("wt1_dense", [DENSE, H1])
        wt2_sb = sb("wt2_sb", [P, H1 // P, H2])
        wt3_sb = sb("wt3_sb", [P, H2 // P])
        bt1_sb = sb("bt1_sb", [P, H1 // P])
        bt2_sb = sb("bt2_sb", [P, H2 // P])
        w1_stage = scaled[:, :, :].rearrange("p a b -> p (a b)").rearrange("p (h n) -> p h n", n=N)
        h1 = scaled[:, :, :].rearrange("p a b -> p (a b)").rearrange("p (c b) -> p c b", b=B)
        h2 = z[:, :, :, :].rearrange("p a b c -> p (a b c)")[:, 0:H2 // P * B].rearrange("p (c b) -> p c b", b=B)
        xb_flat = xb[:, :, :, :].rearrange("p a b c -> p (a b c)")
        fold1 = xb_flat[:, 0:2 * B].rearrange("p (t j b) -> p t j b", t=BT, j=2)
        feat1 = xb_flat[:, 2 * B:3 * B]
        feat2 = xb_flat[:, 3 * B:4 * B]
        fold2 = z[:, :, :, :].rearrange("p a b c -> p (a b c)")[:, 2 * B:4 * B].rearrange(
            "p (t j b) -> p t j b", t=BT, j=2)
        feat2_rows = x_t
        dense_sb = p_full[0:DENSE, :, :].rearrange("p a c -> p (a c)")
        y_sb = p_full[DENSE * 2:DENSE * 2 + 1, :, :].rearrange("p a c -> p (a c)")

        d_bank = [ctx.enter_context(nc.psum_tensor(f"d_bank{i}", [P, HG, N], F32)) for i in range(D_BANKS)]
        a_bank = [ctx.enter_context(nc.psum_tensor(f"a_bank{i}", [P, HG, N], F32)) for i in range(A_BANKS)]
        l1_bank = ctx.enter_context(nc.psum_tensor("l1_bank", [P, C], F32))
        turn_bank = ctx.enter_context(nc.psum_tensor("turn_bank", [P, C], F32))

        ids_in = sem("ids_in")
        w0_in = sem("w0_in")
        w1_in = sem("w1_in")
        tower_in = sem("tower_in")
        dense_in = sem("dense_in")
        gathered = sem("gathered")
        x_rows_out = sem("x_rows_out")
        loaded = [sem("loaded0"), sem("loaded1")]
        y_out = sem("y_out")
        ident_made = sem("ident_made")
        cleared = sem("cleared")
        ids_moved = sem("ids_moved")
        w0_ready = sem("w0_ready")
        w1_hi_ready = sem("w1_hi_ready")
        w1_ready = sem("w1_ready")
        turned = sem("turned")
        turned_out = sem("turned_out")
        e_ready = sem("e_ready")
        x_ready = sem("x_ready")
        z_ready = sem("z_ready")
        l1_done = sem("l1_done")
        p_ready = sem("p_ready")
        p_lo_ready = sem("p_lo_ready")
        d_done = sem("d_done")
        a_done = sem("a_done")
        d_added = sem("d_added")
        a_scaled = sem("a_scaled")
        pool_summed = sem("pool_summed")
        combined = sem("combined")
        folded = sem("folded")
        rows_turned = sem("rows_turned")
        feat2_ready = sem("feat2_ready")
        tower_done = sem("tower_done")
        tower_out = sem("tower_out")

        def there(t):
            return not isinstance(t, int) or t < T

        def wait(eng, semaphore, value):
            if not isinstance(value, int) or value > 0:
                eng.wait_ge(semaphore, value)

        def pool_steps(t, k):
            return 1 + POOL_OPS * t + k

        def over_tiles(eng, pair_of_tiles, between, peeled=1):
            pairs = TPB // 2

            pair_of_tiles(0, 0, True)
            between(1)
            with eng.Fori(1, pairs) as i:
                pair_of_tiles(i, 0, False)
            with eng.Fori(1, BT - 1) as b:
                pair_of_tiles(b * pairs, b, True)
                between(b + 1)
                with eng.Fori(1, pairs) as i:
                    pair_of_tiles(b * pairs + i, b, False)
            pair_of_tiles((BT - 1) * pairs, BT - 1, True)
            with eng.Fori((BT - 1) * pairs + 1, BT * pairs - peeled) as u:
                pair_of_tiles(u, BT - 1, False)
            for u in range(BT * pairs - peeled, BT * pairs):
                pair_of_tiles(u, BT - 1, False)

        block = ctx.enter_context(nc.Block())

        @block.sync
        def _(sp):
            sp.dma_start(ids_all[:, :, :], ids.rearrange("(t p) f -> p t f", p=P)).then_inc(ids_in, 16)
            sp.dma_start(w0[:, :, :], w0_pairs).then_inc(w0_in, 16)
            sp.dma_start(w0b[:, :, :], w0_swapped).then_inc(w0_in, 16)
            sp.dma_start(w0c[:, :], w0_last).then_inc(w0_in, 16)
            sp.dma_start(w1_stage, w1.rearrange("(h m) n -> m h n", m=N)).then_inc(w1_in, 16)
            sp.dma_start(wt1_sb[:, :, :], wt1[0:2 * P, :].rearrange("(k p) n -> p k n", p=P)).then_inc(tower_in, 16)
            sp.dma_start(wt1_dense[:, :], wt1[2 * P:2 * P + DENSE, :]).then_inc(tower_in, 16)
            sp.dma_start(wt2_sb[:, :, :], wt2.rearrange("(k p) n -> p k n", p=P)).then_inc(tower_in, 16)
            with nc.allow_non_contiguous_dma(reason="a few hundred biases and last weights"):
                sp.dma_start(wt3_sb[:, :], wt3.rearrange("(k p) n -> p (k n)", p=P)).then_inc(tower_in, 16)
                sp.dma_start(bt1_sb[:, :], bt1.rearrange("(k p) -> p k", p=P)).then_inc(tower_in, 16)
                sp.dma_start(bt2_sb[:, :], bt2.rearrange("(k p) -> p k", p=P)).then_inc(tower_in, 16)

            def write_x_rows(b):
                sp.wait_ge(turned_out, 2 * b + 2)
                for q in range(4):
                    for row, fields in ((0, F), (F, F // 2)):
                        dst = x_rows[row:row + fields, bass.ds(b * (TPB * C), TPB * C)].rearrange(
                            "(g q) (d b) -> q d g b", q=4, d=D)[q]
                        sp.dma_start(dst, x_t[D * q:D * (q + 1), 0:fields // 4, :]).then_inc(x_rows_out, 16)

            def rolls(first, copies, rows_apart, t):
                cols = x_rows[first:first + F, bass.ds(t * C, C)]
                if copies == 1:
                    return cols
                whole = cols.ap if isinstance(cols.ap, list) else list(cols.ap)
                row, col = list(whole[0]), list(whole[1])
                return bass.AP(cols.tensor, cols.offset, [[rows_apart * row[0], copies], row, col])

            def load(t, par):
                wait(sp, z_ready, Z_OPS * (t - 1))
                sp.wait_ge(x_rows_out, 128 * ((t >> 3) + 1))
                sp.dma_start(xb[:, par, 0, :], rolls(0, 4, 0, t)).then_inc(loaded[par], 16)
                for k in range(CHUNKS):
                    sp.dma_start(xb[:, par, k + 1, :], rolls(4 * k, 4, 1, t)).then_inc(loaded[par], 16)
                sp.dma_start(xb_last[:, par, :], rolls(F // 2, 1, 0, t)).then_inc(loaded[par], 16)

            def pair_of_tiles(u, b, first):
                for par in range(2):
                    if there(2 * u + par + 4):
                        load(2 * u + par + 4, par)

            write_x_rows(0)
            for t in range(4):
                load(t, t % 2)
            over_tiles(sp, pair_of_tiles, write_x_rows, peeled=2)
            sp.wait_ge(combined, COMBINE_OPS * T)
            sp.dma_start(dense_sb, dense_t).then_inc(dense_in, 16)
            sp.wait_ge(tower_out, 2 * (H1 // P + H2 // P + 1))
            sp.dma_start(out.rearrange("b n -> n b"), y_sb).then_inc(y_out, 16)
            sp.wait_ge(y_out, 16)

        @block.gpsimd
        def _(pool):
            nc.gpsimd.memset(ident[:, :], 0.0).then_inc(ident_made, 1)
            pool.wait_ge(ident_made, 1)
            nc.gpsimd.affine_select(out=ident[:, :], in_=ident[:, :], compare_op=ALU.not_equal, fill=1.0,
                                    base=0, pattern=[[-1, P]], channel_multiplier=1).then_inc(ident_made, 1)
            nc.gpsimd.memset(sum1[:, :, :], 0.0).then_inc(cleared, 1)
            pool.wait_ge(ids_in, 16)

            def move_ids(b):
                wait(pool, gathered, 16 * F * b)
                nc.gpsimd.tensor_copy(ids_now[:, :], ids_all[:, bass.ds(b, 1), :].rearrange(
                    "p a f -> p (a f)")).then_inc(ids_moved, 1)

            def gather(b, fields):
                for f in fields:
                    nc.gpsimd.indirect_dma_start(landing[:, f, :], None, tables[f], bass.IndirectOffsetOnAxis(
                        ap=ids_now[:, f:f + 1], axis=0)).then_inc(gathered, 16)

            def free_landing(b):
                wait(pool, e_ready, b)
                wait(pool, turned, 2 * b)

            def add(out_, in0, in1):
                nc.gpsimd.tensor_tensor(out_, in0, in1, ALU.add).then_inc(pool_summed, 1)

            def sum_layer1(t, b, par):
                acc = sum1[:, bass.ds(b, 1), :].rearrange("p a c -> p (a c)")
                add(acc, acc, p_full[:, par, :])

            def tile(t, b_next, par, ids_for=None):
                if ids_for is not None:
                    pool.wait_ge(ids_moved, ids_for + 1)
                for j in range(DG):
                    ring = HALF * (j % 2)
                    at = 3 * j
                    for half in range(2):
                        pool.wait_ge(a_scaled, A_GROUPS * t + HALF * j + 2 * half + 2)
                        if half == 0:
                            wait(pool, pool_summed, pool_steps(t, at))
                        add(pair[:, half, :], scaled[:, ring + 2 * half, :], scaled[:, ring + 2 * half + 1, :])
                    pool.wait_ge(pool_summed, pool_steps(t, at + 2))
                    add(a_sum[:, j, :], pair[:, 0, :], pair[:, 1, :])
                pool.wait_ge(pool_summed, pool_steps(t, 3 * DG))
                add(a_fold[:, :, :], a_sum[:, :, 0:2 * N], a_sum[:, :, 2 * N:4 * N])
                pool.wait_ge(pool_summed, pool_steps(t, 3 * DG + 1))
                wait(pool, combined, COMBINE_OPS * (t - 1))
                if there(t + 1):
                    pool.wait_ge(p_ready, 2 * (t + 2))
                add(a_part[:, par, :, :], a_fold[:, :, 0:N], a_fold[:, :, N:2 * N])
                if there(t + 1):
                    sum_layer1(t + 1, b_next, 1 - par)

            move_ids(0)
            pool.wait_ge(ids_moved, 1)
            gather(0, range(F))
            free_landing(1)
            move_ids(1)
            pool.wait_ge(ids_moved, 2)
            gather(1, range(F))
            pool.wait_ge(cleared, 1)
            pool.wait_ge(p_ready, 2)
            sum_layer1(0, 0, 0)

            after = {3: range(0, 8), 4: range(8, 16), 5: range(16, 24), 6: range(24, 32)}

            def b_tile(b, ahead):
                for k in range(TPB):
                    tile(b * TPB + k, b + (k + 1) // TPB, k % 2, b + 2 if ahead and k == 3 else None)
                    if ahead and k == 2:
                        free_landing(b + 2)
                        move_ids(b + 2)
                    if ahead and k in after:
                        gather(b + 2, after[k])

            b_tile(0, True)
            with pool.Fori(1, BT - 2) as b:
                b_tile(b, True)
            b_tile(BT - 2, False)
            b_tile(BT - 1, False)

        @block.scalar
        def _(act):
            act.wait_ge(w1_in, 16)
            nc.scalar.activation(w1h[:, :, :], w1_stage, ACT.Copy).then_inc(w1_hi_ready, 1)

            def turn_out(b):
                wait(act, x_rows_out, 128 * b)
                for half, bank in enumerate((turn_bank, l1_bank)):
                    act.wait_ge(turned, 2 * b + half + 1)
                    nc.scalar.activation(x_t[:, half * DG:(half + 1) * DG, :].rearrange("p g b -> p (g b)"),
                                         bank[:, :], ACT.Copy).then_inc(turned_out, 1)
                act.wait_ge(gathered, 16 * F * (b + 1))
                ring = e_ring[:, bass.ds((b & 1) * TPB, TPB), :].rearrange("p g (j f) -> p (g j) f", f=F)
                nc.scalar.activation(ring, landing[:, :, :].rearrange("p f d -> p d f"),
                                     ACT.Copy).then_inc(e_ready, 1)

            def layer1_out(t, par):
                act.wait_ge(l1_done, t + 1)
                wait(act, p_lo_ready, t - 1)
                nc.scalar.activation(p_hi[:, par, :], l1_bank[:, :], ACT.Relu).then_inc(p_ready, 1)
                nc.scalar.activation(p_full[:, par, :], l1_bank[:, :], ACT.Relu).then_inc(p_ready, 1)

            def tile(t, par):
                act.wait_ge(x_ready, t + 1)
                for j in range(DG):
                    wait(act, pool_summed, pool_steps(t, 3 * j - 4) if j >= 2 or not isinstance(t, int) or t
                         else 0)
                    for g in range(HALF):
                        act.wait_ge(a_done, A_GROUPS * t + HALF * j + g + 1)
                        for h in range(HG):
                            field = HG * (2 * g + 1) + h
                            last = nc.scalar.activation(
                                scaled[:, HALF * (j % 2) + g, h * N:(h + 1) * N], a_bank[g % 2][:, h, :],
                                ACT.Copy, scale=x_now[:, par, j, field:field + 1])
                        last.then_inc(a_scaled, 1)
                        if (j, g) == (1, 3) and there(t + 1):
                            layer1_out(t + 1, 1 - par)

            def pair_of_tiles(u, b, first):
                for par in range(2):
                    tile(2 * u + par, par)

            turn_out(0)
            layer1_out(0, 0)
            act.wait_ge(w1_ready, 1)
            over_tiles(act, pair_of_tiles, turn_out)

            act.wait_ge(tower_in, 6 * 16)
            for half in range(2):
                act.wait_ge(rows_turned, half + 1)
                nc.scalar.activation(feat2[:, half * HALF_B:(half + 1) * HALF_B], (turn_bank, l1_bank)[half][:, :],
                                     ACT.Copy).then_inc(feat2_ready, 1)
            act.wait_ge(pool_summed, pool_steps(T - 1, POOL_OPS - 1))
            step = 0
            for half in range(2):
                cols = slice(half * HALF_B, (half + 1) * HALF_B)
                for c in range(H1 // P):
                    step += 1
                    act.wait_ge(tower_done, step)
                    nc.scalar.activation(h1[:, c, cols], d_bank[step % 2][:, :, :].rearrange("p a b -> p (a b)"),
                                         ACT.Relu, bias=bt1_sb[:, c:c + 1]).then_inc(tower_out, 1)
            for half in range(2):
                cols = slice(half * HALF_B, (half + 1) * HALF_B)
                for c in range(H2 // P):
                    step += 1
                    act.wait_ge(tower_done, step)
                    nc.scalar.activation(h2[:, c, cols], d_bank[step % 2][:, :, :].rearrange("p a b -> p (a b)"),
                                         ACT.Relu, bias=bt2_sb[:, c:c + 1]).then_inc(tower_out, 1)
            for half in range(2):
                cols = slice(half * HALF_B, (half + 1) * HALF_B)
                step += 1
                act.wait_ge(tower_done, step)
                nc.scalar.activation(y_sb[:, cols], d_bank[step % 2][0:1, :, :].rearrange("p a b -> p (a b)"),
                                     ACT.Copy).then_inc(tower_out, 1)

        @block.vector
        def _(dve):
            nc.vector.memset(sum2[:, :, :, :], 0.0).then_inc(cleared, 1)
            dve.wait_ge(w0_in, 48)
            flat = "p k n -> p (k n)"
            nc.vector.tensor_tensor(w0[:, 1:CHUNKS, :].rearrange(flat), w0[:, 1:CHUNKS, :].rearrange(flat),
                                    w0b[:, 1:CHUNKS, :].rearrange(flat), ALU.add)
            for q in range(1, 4):
                rows = slice(F * q, F * (q + 1))
                last = nc.vector.tensor_tensor(w0[rows, 0, :], w0[rows, 0, :], w0b[rows, 0, :], ALU.add)
            last.then_inc(w0_ready, 1)
            dve.wait_ge(w1_hi_ready, 1)
            nc.vector.tensor_tensor(w1l[:, :, :], w1_stage, w1h[:, :, :].bitcast(F32),
                                    ALU.subtract).then_inc(w1_ready, 1)
            dve.wait_ge(cleared, 2)

            def copy_x(t, par):
                wait(dve, a_scaled, A_GROUPS * (t - 1))
                wait(dve, d_added, D_OPS * (t - 1))
                nc.vector.tensor_copy(x_now[:, par, :, :].rearrange("p j f -> p (j f)"),
                                      e_ring[:, bass.ds(t & (2 * TPB - 1), 1), :].rearrange("p a c -> p (a c)")
                                      ).then_inc(x_ready, 1)

            def products(t, u, k, par):
                if k == 0:
                    dve.wait_ge(loaded[par], 96 * (u + 1))
                    wait(dve, l1_done, t - 1)
                if k < CHUNKS:
                    nc.vector.tensor_tensor(z[:, par, k, :], xb[:, par, 0, :], xb[:, par, k + 1, :],
                                            ALU.mult).then_inc(z_ready, 1)
                else:
                    nc.vector.tensor_tensor(z_last[:, par, :], xb[0:F, par, 0, :], xb_last[:, par, :],
                                            ALU.mult).then_inc(z_ready, 1)

            def low_part(t, par):
                dve.wait_ge(p_ready, 2 * (t + 1))
                nc.vector.tensor_tensor(p_lo[:, par, :], p_full[:, par, :], p_hi[:, par, :].bitcast(F32),
                                        ALU.subtract).then_inc(p_lo_ready, 1)

            def combine(t, b, par, step):
                if step == 0:
                    dve.wait_ge(d_added, D_OPS * (t + 1))
                    wait(dve, combined, COMBINE_OPS * t)
                    nc.vector.tensor_tensor(d_fold[:, :, :], d_part[:, par, :, 0, :], d_part[:, par, :, 1, :],
                                            ALU.add).then_inc(combined, 1)
                elif step == 1:
                    dve.wait_ge(combined, COMBINE_OPS * t + 1)
                    dve.wait_ge(pool_summed, pool_steps(t, POOL_OPS - 1))
                    nc.vector.tensor_tensor(cur[:, :, :], d_fold[:, :, :], a_part[:, par, :, :],
                                            ALU.add).then_inc(combined, 1)
                else:
                    dve.wait_ge(combined, COMBINE_OPS * t + 2)
                    acc = sum2[:, bass.ds(b, 1), :, :].rearrange("p a j n -> p (a j n)")
                    nc.vector.scalar_tensor_tensor(out=acc, in0=cur[:, :, :].rearrange("p j n -> p (j n)"),
                                                   scalar=0.0, in1=acc, op0=ALU.max,
                                                   op1=ALU.add).then_inc(combined, 1)

            def tile(t, u, par, b_before):
                dve.wait_ge(x_ready, t + 1)
                wait(dve, combined, COMBINE_OPS * (t - 1))
                for j in range(DG):
                    for g in range(HALF):
                        at = HALF * j + g
                        dve.wait_ge(d_done, DG * HALF * t + at + 1)
                        for h in range(HG):
                            op = HG * at + h
                            field = HG * 2 * g + h
                            src = d_bank[at % D_BANKS][:, h, :]
                            acc = d_part[:, par, j, h % 2, :]
                            x = x_now[:, par, j, field:field + 1]
                            if g == 0 and h < 2:
                                nc.vector.tensor_scalar(acc, src, x, None, ALU.mult).then_inc(d_added, 1)
                            else:
                                dve.wait_ge(d_added, D_OPS * t + op - 1)
                                nc.vector.scalar_tensor_tensor(out=acc, in0=src, scalar=x, in1=acc,
                                                               op0=ALU.mult, op1=ALU.add).then_inc(d_added, 1)
                        if there(t + 2) and at in (0, 2, 4, 6, 8):
                            products(t + 2, u + 1, at // 2, par)
                        if there(t + 1) and at == 3:
                            copy_next(t + 1, u, par)
                        if at in (9, 10, 11) and not (isinstance(t, int) and t == 0):
                            combine(t - 1, b_before, 1 - par, at - 9)
                        if there(t + 1) and at == 12:
                            low_part(t + 1, 1 - par)

            def copy_next(t, u, par):
                dve.wait_ge(e_ready, (t >> 3) + 1)
                copy_x(t, 1 - par)

            def pair_of_tiles(u, b, first):
                for par in range(2):
                    tile(2 * u + par, u, par, b - 1 if first and par == 0 else b)

            dve.wait_ge(e_ready, 1)
            copy_x(0, 0)
            for t in range(2):
                for k in range(Z_OPS):
                    products(t, 0, k, t)
            low_part(0, 0)
            over_tiles(dve, pair_of_tiles, lambda b: None)
            for step in range(COMBINE_OPS):
                combine(T - 1, BT - 1, 1, step)

            dve.wait_ge(combined, COMBINE_OPS * T)
            nc.vector.tensor_tensor(fold2, sum2[:, :, 0:2, :], sum2[:, :, 2:4, :], ALU.add).then_inc(folded, 1)
            dve.wait_ge(folded, 1)
            nc.vector.tensor_tensor(feat2_rows[:, :, :], fold2[:, :, 0, :], fold2[:, :, 1, :],
                                    ALU.add).then_inc(folded, 1)
            dve.wait_ge(pool_summed, pool_steps(T - 1, POOL_OPS - 1))
            by_d = sum1[:, :, :].rearrange("p t (j b) -> p t j b", j=DG)
            nc.vector.tensor_tensor(fold1, by_d[:, :, 0:2, :], by_d[:, :, 2:4, :], ALU.add).then_inc(folded, 1)
            dve.wait_ge(folded, 3)
            nc.vector.tensor_tensor(feat1.rearrange("p (t b) -> p t b", t=BT), fold1[:, :, 0, :],
                                    fold1[:, :, 1, :], ALU.add).then_inc(folded, 1)

        @block.tensor
        def _(pe):
            def transposes(b):
                pe.wait_ge(gathered, 16 * F * (b + 1))
                wait(pe, turned_out, 2 * b)
                for half, bank in enumerate((turn_bank, l1_bank)):
                    for k in range(4):
                        f = 4 * (half * 4 + k)
                        last = nc.tensor.transpose(bank[:, k * P:(k + 1) * P],
                                                   landing[:, f:f + 4, :].rearrange("p f d -> p (f d)"),
                                                   ident[:, :])
                    last.then_inc(turned, 1)

            def layer1(t, k, par):
                pe.wait_ge(z_ready, Z_OPS * t + k + 1)
                if k < CHUNKS:
                    last = nc.tensor.matmul(l1_bank[:, :], w0[:, k, :], z[:, par, k, :], start=k == 0, stop=False)
                else:
                    last = nc.tensor.matmul(l1_bank[:, :], w0c[:, :], z_last[:, par, :], start=False, stop=True)
                    last.then_inc(l1_done, 1)

            def group(bank, j, h, par):
                cols = slice(j * P, (j + 1) * P)
                o = bank[:, :, :].rearrange("p a b -> p (a b)")
                hi = w1h[:, h:h + HG, :].rearrange("p a b -> p (a b)")
                lo = w1l[:, h:h + HG, :].rearrange("p a b -> p (a b)")
                nc.tensor.matmul(o, p_hi[:, par, cols], hi, start=True, stop=False)
                nc.tensor.matmul(o, p_hi[:, par, cols], lo, start=False, stop=False)
                return nc.tensor.matmul(o, p_lo[:, par, cols], hi, start=False, stop=True)

            def tile(t, b_turned, par):
                pe.wait_ge(p_ready, 2 * t + 2)
                pe.wait_ge(p_lo_ready, t + 1)
                for at in range(DG * HALF):
                    j, g = at // HALF, at % HALF
                    wait(pe, d_added, D_OPS * t + HG * (at + 1 - D_BANKS))
                    group(d_bank[at % D_BANKS], j, 2 * HG * g, par).then_inc(d_done, 1)
                    wait(pe, a_scaled, A_GROUPS * t + at + 1 - A_BANKS)
                    group(a_bank[at % A_BANKS], j, 2 * HG * g + HG, par).then_inc(a_done, 1)
                    if there(t + 1) and 1 <= at < 1 + Z_OPS:
                        if at == 1:
                            pe.wait_ge(turned_out, 2 * (b_turned + 1))
                        layer1(t + 1, at - 1, 1 - par)

            def pair_of_tiles(u, b, first):
                for par in range(2):
                    tile(2 * u + par, b if first or (isinstance(b, int) and b == BT - 1) else b + 1, par)

            pe.wait_ge(ident_made, 2)
            transposes(0)
            pe.wait_ge(turned_out, 2)
            pe.wait_ge(w0_ready, 1)
            for k in range(Z_OPS):
                layer1(0, k, 0)
            pe.wait_ge(w1_ready, 1)
            over_tiles(pe, pair_of_tiles, transposes)

            pe.wait_ge(folded, 2)
            for half, bank in enumerate((turn_bank, l1_bank)):
                for k in range(DG):
                    last = nc.tensor.transpose(bank[:, k * P:(k + 1) * P], feat2_rows[:, half * DG + k, :],
                                               ident[:, :])
                last.then_inc(rows_turned, 1)
            pe.wait_ge(folded, 4)
            pe.wait_ge(dense_in, 16)
            pe.wait_ge(feat2_ready, 2)
            pe.wait_ge(tower_in, 6 * 16)
            step = 0

            def bank_of(step, rows):
                wait(pe, tower_out, step - 2)
                return d_bank[step % 2][0:rows, :, :].rearrange("p a b -> p (a b)")

            for half in range(2):
                cols = slice(half * HALF_B, (half + 1) * HALF_B)
                for c in range(H1 // P):
                    step += 1
                    o, n = bank_of(step, P), slice(c * P, (c + 1) * P)
                    nc.tensor.matmul(o, wt1_sb[:, 0, n], feat1[:, cols], start=True, stop=False)
                    nc.tensor.matmul(o, wt1_sb[:, 1, n], feat2[:, cols], start=False, stop=False)
                    nc.tensor.matmul(o, wt1_dense[:, n], dense_sb[:, cols], start=False,
                                     stop=True).then_inc(tower_done, 1)
            for half in range(2):
                cols = slice(half * HALF_B, (half + 1) * HALF_B)
                pe.wait_ge(tower_out, (half + 1) * (H1 // P))
                for c in range(H2 // P):
                    step += 1
                    o = bank_of(step, P)
                    for k in range(H1 // P):
                        last = nc.tensor.matmul(o, wt2_sb[:, k, c * P:(c + 1) * P], h1[:, k, cols],
                                                start=k == 0, stop=k == H1 // P - 1)
                    last.then_inc(tower_done, 1)
            for half in range(2):
                cols = slice(half * HALF_B, (half + 1) * HALF_B)
                pe.wait_ge(tower_out, 2 * (H1 // P) + (half + 1) * (H2 // P))
                step += 1
                o = bank_of(step, 1)
                for k in range(H2 // P):
                    last = nc.tensor.matmul(o, wt3_sb[:, k:k + 1], h2[:, k, cols], start=k == 0,
                                            stop=k == H2 // P - 1)
                last.then_inc(tower_done, 1)


def kernel(**inputs):
    import numpy as np
    import concourse.bacc as bacc
    from concourse.bass_utils import run_bass_kernel_spmd

    own = np.arange(F)
    w0 = np.asarray(inputs["L0_rec_filter_0"])[0]
    shift = np.arange(4 * CHUNKS)
    other = (own[None, :] + shift[:, None]) % F

    def chunked(rows):
        return np.ascontiguousarray(w0[rows.ravel()].reshape(CHUNKS, P, N).transpose(1, 0, 2))

    arrays = {
        "dense_t": np.ascontiguousarray(np.asarray(inputs["dense_ctx"]).T),
        "ids": np.ascontiguousarray(inputs["ids"]),
        "w0_pairs": chunked(own[None, :] * F + other),
        "w0_swapped": chunked(other * F + own[None, :]),
        "w0_last": np.ascontiguousarray(w0[own * F + (own + F // 2) % F]),
        "w1": np.ascontiguousarray(np.asarray(inputs["L0_rec_filter_1"])[0]),
        "wt1": np.ascontiguousarray(inputs["W_top1"]), "bt1": np.ascontiguousarray(inputs["b_top1"]),
        "wt2": np.ascontiguousarray(inputs["W_top2"]), "bt2": np.ascontiguousarray(inputs["b_top2"]),
        "wt3": np.ascontiguousarray(inputs["W_top3"]),
    }
    tables = {f"tbl_{f}": np.ascontiguousarray(inputs[f"tbl_{f}"]) for f in range(F)}
    nc = bacc.Bacc("TRN2", target_bir_lowering=False, num_devices=1)

    def declare(name, a):
        return nc.dram_tensor(f"in_{name}", a.shape, mybir.dt.from_np(a.dtype), kind="ExternalInput").ap()

    args = {name: declare(name, a) for name, a in arrays.items()}
    args["tables"] = [declare(name, a) for name, a in tables.items()]
    args["out"] = nc.dram_tensor("out_y", (B, 1), F32, kind="ExternalOutput").ap()
    build_cin_tower(nc, **args)
    fed = {f"in_{name}": a for name, a in {**arrays, **tables}.items()}
    r = run_bass_kernel_spmd(nc, [fed], core_ids=[0])
    return r.results[0]["out_y"]
```

```python
import concourse.bass as bass
from concourse import mybir
from contextlib import ExitStack

F32 = mybir.dt.float32
F32R = mybir.dt.float32r
I32 = mybir.dt.int32
ALU = mybir.AluOpType
ACT = mybir.ActivationFunctionType

B, F, D = 1024, 32, 32
N = 128
P = 128
BT = B // P
DG = 4
TPB = D // DG
T = BT * TPB
C = DG * P
CHUNKS = 4
HG = C // N
GROUPS = F // HG
HALF = GROUPS // 2
D_BANKS, A_BANKS = 4, 3
PAIRS = DG * HALF
Z_OPS = CHUNKS + 1
Z_AT, ZL_AT = (0, 1, 3, 4), (6, 7, 8, 9, 10)
X_AT, P_LO_AT, SUM2_AT, SUM1_AT = 5, 11, 13, 12
SQUARE_AT, ZH_AT = (0, 1, 2), (4, 5, 6, 7)
P_AT = 10
IN_PLACE_AT = (2,8,12)
L1_AT = (0,2,2,2,2,2,1,1,1)
POOL_OPS = 3 * DG + 2
AHEAD_FROM = 2
SQUARES = 3
H1, H2, DENSE = 512, 256, 16
HALF_B = 512


def build_cin_tower(nc, dense_t, ids, tables, w0_pairs, w0_swapped, w0_last, w1, wt1, bt1, wt2, bt2, wt3, out):
    ctx = ExitStack()
    with ctx:
        def sb(name, shape, dt=F32):
            return ctx.enter_context(nc.sbuf_tensor(name, shape, dt))

        def sem(name):
            return ctx.enter_context(nc.semaphore(name))

        x_rows = nc.dram_tensor("x_rows", (F + F // 2, T * C), F32, kind="Internal").ap()

        w1h = sb("w1h", [P, F, N], F32R)
        w1l = sb("w1l", [P, F, N], F32R)
        w0h = sb("w0h", [P, CHUNKS, N], F32R)
        w0l = sb("w0l", [P, CHUNKS, N], F32R)
        w0_stack = sb("w0_stack", [3 * F, N], F32R)
        ident = sb("ident", [P, P])
        ids_all = sb("ids_all", [P, BT, F], I32)
        ids_now = sb("ids_now", [P, F], I32)
        landing = sb("landing", [P, F, D])
        e_ring = sb("e_ring", [P, 2 * TPB, C // DG])
        x_t = sb("x_t", [P, F // 4, P])
        xb = sb("xb", [P, 2, CHUNKS + 1, C])
        z = sb("z", [P, CHUNKS, C])
        z_last = sb("z_last", [F, C])
        z_hi = sb("z_hi", [P, 2, CHUNKS, C], F32R)
        z_lo = sb("z_lo", [P, 2, CHUNKS, C], F32R)
        z_stack = sb("z_stack", [3 * F, 2, C], F32R)
        p_hi = sb("p_hi", [P, 2, C], F32R)
        p_lo = sb("p_lo", [P, 2, C], F32R)
        x_now = sb("x_now", [P, 2, DG, F])
        scaled = sb("scaled", [P, 2 * HALF, HG * N])
        mixed = sb("mixed", [P, 2 * HALF, HG * N])
        pair = sb("pair", [P, 2, HG * N])
        a_sum = sb("a_sum", [P, DG, HG * N])
        a_fold = sb("a_fold", [P, DG, 2 * N])
        a_part = sb("a_part", [P, 2, DG, N])
        sum1 = sb("sum1", [P, 2 * C])
        zeros = sb("zeros", [P, C])
        sum2 = sb("sum2", [P, DG * N])
        fold1 = sb("fold1", [P, C // 2])
        fold2 = sb("fold2", [P, DG * N // 2])
        feat1 = sb("feat1", [P, BT, P])
        feat2_rows = sb("feat2_rows", [P, BT, N])
        wt3_sb = sb("wt3_sb", [P, H2 // P])
        bt1_sb = sb("bt1_sb", [P, H1 // P])
        bt2_sb = sb("bt2_sb", [P, H2 // P])
        flat = "p a b -> p (a b)"
        w1_stage = scaled[:, :, :].rearrange(flat).rearrange("p (h n) -> p h n", n=N)
        mixed_flat = mixed[:, :, :].rearrange(flat)
        w0 = mixed_flat[:, 0:CHUNKS * N]
        w0b = mixed_flat[:, CHUNKS * N:2 * CHUNKS * N]
        w0c = mixed_flat[0:F, 2 * CHUNKS * N:2 * CHUNKS * N + N]
        h1 = scaled[:, :, :].rearrange(flat).rearrange("p (c b) -> p c b", b=B)
        h2 = mixed_flat[:, 0:H2 // P * B].rearrange("p (c b) -> p c b", b=B)
        feat2 = mixed_flat[:, H2 // P * B:(H2 // P + 1) * B]
        wt1_sb = landing[:, :, :].rearrange(flat).rearrange("p (k n) -> p k n", n=H1)
        wt1_dense = x_t[0:DENSE, :, :].rearrange(flat)[:, 0:H1]
        wt2_sb = e_ring[:, 0:TPB, :].rearrange(flat).rearrange("p (k n) -> p k n", n=H2)
        feat1_cols = feat1[:, :, :].rearrange(flat)
        dense_sb = pair[0:DENSE, :, :].rearrange(flat)
        y_sb = pair[DENSE * 2:DENSE * 2 + 1, :, :].rearrange(flat)

        d_bank = [ctx.enter_context(nc.psum_tensor(f"d_bank{i}", [P, HG, N], F32)) for i in range(D_BANKS)]
        a_bank = [ctx.enter_context(nc.psum_tensor(f"a_bank{i}", [P, HG, N], F32)) for i in range(A_BANKS)]
        l1_bank = ctx.enter_context(nc.psum_tensor("l1_bank", [P, C], F32))
        turn_banks = (a_bank[2][:, :, :].rearrange(flat), l1_bank[:, :])

        ids_in = sem("ids_in")
        w0_in = sem("w0_in")
        w1_in = sem("w1_in")
        tower_in = sem("tower_in")
        dense_in = sem("dense_in")
        gathered = sem("gathered")
        x_rows_out = sem("x_rows_out")
        loaded = [sem("loaded0"), sem("loaded1")]
        y_out = sem("y_out")
        ident_made = sem("ident_made")
        ids_moved = sem("ids_moved")
        w0_summed = sem("w0_summed")
        w0_hi_ready = sem("w0_hi_ready")
        w0_ready = sem("w0_ready")
        w1_hi_ready = sem("w1_hi_ready")
        w1_ready = sem("w1_ready")
        turned = sem("turned")
        turned_out = sem("turned_out")
        e_ready = sem("e_ready")
        x_ready = sem("x_ready")
        z_ready = sem("z_ready")
        z_hi_ready = sem("z_hi_ready")
        squared = sem("squared")
        z_lo_ready = sem("z_lo_ready")
        l1_done = sem("l1_done")
        p_ready = sem("p_ready")
        p_lo_ready = sem("p_lo_ready")
        d_done = sem("d_done")
        a_done = sem("a_done")
        in_place = sem("in_place")
        sum1_cleared = sem("sum1_cleared")
        sum1_added = sem("sum1_added")
        d_added = sem("d_added")
        a_scaled = sem("a_scaled")
        pool_summed = sem("pool_summed")
        combined = sem("combined")
        rows_folded = sem("rows_folded")
        cols_folded = sem("cols_folded")
        rows_turned = sem("rows_turned")
        feat2_ready = sem("feat2_ready")
        tower_done = sem("tower_done")
        tower_out = sem("tower_out")

        def there(t):
            return not isinstance(t, int) or t < T

        def wait(eng, semaphore, value):
            if not isinstance(value, int) or value > 0:
                eng.wait_ge(semaphore, value)

        def bank(par, at, banks):
            n = PAIRS * par + at
            return n % banks, next(d for d in range(1, 2 * PAIRS) if (n - d) % (2 * PAIRS) % banks == n % banks)

        def pool_steps(t, k):
            return POOL_OPS * t + k

        def over_tiles(eng, pair_of_tiles, between, peeled=1):
            pairs = TPB // 2

            pair_of_tiles(0, 0, True)
            between(1)
            with eng.Fori(1, pairs) as i:
                pair_of_tiles(i, 0, False)
            with eng.Fori(1, BT - 1) as b:
                pair_of_tiles(b * pairs, b, True)
                between(b + 1)
                with eng.Fori(1, pairs) as i:
                    pair_of_tiles(b * pairs + i, b, False)
            pair_of_tiles((BT - 1) * pairs, BT - 1, True)
            with eng.Fori((BT - 1) * pairs + 1, BT * pairs - peeled) as u:
                pair_of_tiles(u, BT - 1, False)
            for u in range(BT * pairs - peeled, BT * pairs):
                pair_of_tiles(u, BT - 1, False)

        block = ctx.enter_context(nc.Block())

        @block.sync
        def _(sp):
            sp.dma_start(ids_all[:, :, :], ids.rearrange("(t p) f -> p t f", p=P)).then_inc(ids_in, 16)
            sp.dma_start(w0, w0_pairs.rearrange("p k n -> p (k n)")).then_inc(w0_in, 16)
            sp.dma_start(w0b, w0_swapped.rearrange("p k n -> p (k n)")).then_inc(w0_in, 16)
            sp.dma_start(w0c, w0_last).then_inc(w0_in, 16)
            sp.dma_start(w1_stage, w1.rearrange("(h m) n -> m h n", m=N)).then_inc(w1_in, 16)
            with nc.allow_non_contiguous_dma(reason="a few hundred biases and last weights"):
                sp.dma_start(wt3_sb[:, :], wt3.rearrange("(k p) n -> p (k n)", p=P)).then_inc(tower_in, 16)
                sp.dma_start(bt1_sb[:, :], bt1.rearrange("(k p) -> p k", p=P)).then_inc(tower_in, 16)
                sp.dma_start(bt2_sb[:, :], bt2.rearrange("(k p) -> p k", p=P)).then_inc(tower_in, 16)

            def write_x_rows(b):
                sp.wait_ge(turned_out, 2 * b + 2)
                for q in range(4):
                    for row, fields in ((0, F), (F, F // 2)):
                        dst = x_rows[row:row + fields, bass.ds(b * (TPB * C), TPB * C)].rearrange(
                            "(g q) (d b) -> q d g b", q=4, d=D)[q]
                        sp.dma_start(dst, x_t[D * q:D * (q + 1), 0:fields // 4, :]).then_inc(x_rows_out, 16)

            def rolls(first, copies, rows_apart, t):
                cols = x_rows[first:first + F, bass.ds(t * C, C)]
                whole = cols.ap if isinstance(cols.ap, list) else list(cols.ap)
                row, col = list(whole[0]), list(whole[1])
                return bass.AP(cols.tensor, cols.offset, [[rows_apart * row[0], copies], row, col])

            def load(t, par):
                wait(sp, z_lo_ready, Z_OPS * (t - 1))
                sp.wait_ge(x_rows_out, 128 * ((t >> 3) + 1))
                sp.dma_start(xb[:, par, 0, :], rolls(0, 4, 0, t)).then_inc(loaded[par], 16)
                for k in range(CHUNKS):
                    sp.dma_start(xb[:, par, k + 1, :], rolls(4 * k + 1, 4, 1, t)).then_inc(loaded[par], 16)

            def pair_of_tiles(u, b, first):
                for par in range(2):
                    if there(2 * u + par + 4):
                        load(2 * u + par + 4, par)

            write_x_rows(0)
            for t in range(4):
                load(t, t % 2)
            over_tiles(sp, pair_of_tiles, write_x_rows, peeled=2)
            sp.wait_ge(x_ready, T)
            sp.wait_ge(turned, 2 * BT)
            sp.wait_ge(x_rows_out, 128 * BT)
            sp.dma_start(wt1_sb[:, :, :], wt1[0:2 * P, :].rearrange("(k p) n -> p k n", p=P)).then_inc(tower_in, 16)
            sp.dma_start(wt1_dense[:, :], wt1[2 * P:2 * P + DENSE, :]).then_inc(tower_in, 16)
            sp.dma_start(wt2_sb[:, :, :], wt2.rearrange("(k p) n -> p k n", p=P)).then_inc(tower_in, 16)
            sp.wait_ge(pool_summed, pool_steps(T - 1, POOL_OPS))
            sp.dma_start(dense_sb, dense_t).then_inc(dense_in, 16)
            sp.wait_ge(tower_out, 2 * (H1 // P + H2 // P + 1))
            sp.dma_start(out.rearrange("b n -> n b"), y_sb).then_inc(y_out, 16)
            sp.wait_ge(y_out, 16)

        @block.gpsimd
        def _(pool):
            nc.gpsimd.memset(ident[:, :], 0.0).then_inc(ident_made, 1)
            pool.wait_ge(ident_made, 1)
            nc.gpsimd.affine_select(out=ident[:, :], in_=ident[:, :], compare_op=ALU.not_equal, fill=1.0,
                                    base=0, pattern=[[-1, P]], channel_multiplier=1).then_inc(ident_made, 1)
            pool.wait_ge(ids_in, 16)

            def move_ids(b):
                wait(pool, gathered, 16 * F * b)
                nc.gpsimd.tensor_copy(ids_now[:, :], ids_all[:, bass.ds(b, 1), :].rearrange(
                    "p a f -> p (a f)")).then_inc(ids_moved, 1)

            def gather(b, fields):
                for f in fields:
                    nc.gpsimd.indirect_dma_start(landing[:, f, :], None, tables[f], bass.IndirectOffsetOnAxis(
                        ap=ids_now[:, f:f + 1], axis=0)).then_inc(gathered, 16)

            def free_landing(b):
                wait(pool, e_ready, b)
                wait(pool, turned, 2 * b)

            def add(out_, in0, in1):
                nc.gpsimd.tensor_tensor(out_, in0, in1, ALU.add).then_inc(pool_summed, 1)

            def tile(t, b, k, ahead, late):
                par = k % 2
                for j in range(DG):
                    if ahead and (k, j) == (AHEAD_FROM, 2):
                        pool.wait_ge(ids_moved, b + 3)
                    ring = HALF * (j % 2)
                    at = 3 * j
                    for half in range(2):
                        pool.wait_ge(d_added, PAIRS * t + HALF * j + 2 * half + 2)
                        if half == 0:
                            wait(pool, pool_summed, pool_steps(t, at))
                        add(pair[:, half, :], mixed[:, ring + 2 * half, :], mixed[:, ring + 2 * half + 1, :])
                    pool.wait_ge(pool_summed, pool_steps(t, at + 2))
                    add(a_sum[:, j, :], pair[:, 0, :], pair[:, 1, :])
                    if ahead and (k, j) == (AHEAD_FROM, 1):
                        free_landing(b + 2)
                        move_ids(b + 2)
                    if k >= AHEAD_FROM and ahead:
                        gather(b + 2, at_slot.get((k, j), ()))
                    if k == 0 and late:
                        gather(b + 1, at_slot.get((k, j), ()))
                pool.wait_ge(pool_summed, pool_steps(t, 3 * DG))
                add(a_fold[:, :, :], a_sum[:, :, 0:2 * N], a_sum[:, :, 2 * N:4 * N])
                pool.wait_ge(pool_summed, pool_steps(t, 3 * DG + 1))
                wait(pool, combined, t - 1)
                add(a_part[:, par, :, :], a_fold[:, :, 0:N], a_fold[:, :, N:2 * N])

            move_ids(0)
            pool.wait_ge(ids_moved, 1)
            gather(0, range(F))
            free_landing(1)
            move_ids(1)
            pool.wait_ge(ids_moved, 2)
            gather(1, range(F))

            slots = [(k, j) for k in (*range(AHEAD_FROM, TPB), 0) for j in range(DG)][2:]
            at_slot = {slot: range(F * n // len(slots), F * (n + 1) // len(slots)) for n, slot in enumerate(slots)}

            def b_tile(b, ahead, late):
                for k in range(TPB):
                    tile(b * TPB + k, b, k, ahead, late)

            b_tile(0, True, False)
            with pool.Fori(1, BT - 2) as b:
                b_tile(b, True, True)
            b_tile(BT - 2, False, True)
            b_tile(BT - 1, False, False)

        @block.scalar
        def _(act):
            act.wait_ge(w0_summed, 1)
            nc.scalar.activation(w0h[:, :, :].rearrange(flat), w0, ACT.Copy)
            for q in range(2):
                last = nc.scalar.activation(w0_stack[F * q:F * (q + 1), :], w0c, ACT.Copy)
            last.then_inc(w0_hi_ready, 1)
            act.wait_ge(w1_in, 16)
            nc.scalar.activation(w1h[:, :, :], w1_stage, ACT.Copy).then_inc(w1_hi_ready, 1)

            def turn_out(b):
                wait(act, x_rows_out, 128 * b)
                for half, turn in enumerate(turn_banks):
                    act.wait_ge(turned, 2 * b + half + 1)
                    nc.scalar.activation(x_t[:, half * DG:(half + 1) * DG, :].rearrange("p g b -> p (g b)"),
                                         turn, ACT.Copy).then_inc(turned_out, 1)
                act.wait_ge(gathered, 16 * F * (b + 1))
                ring = e_ring[:, bass.ds((b & 1) * TPB, TPB), :].rearrange("p g (j f) -> p (g j) f", f=F)
                nc.scalar.activation(ring, landing[:, :, :].rearrange("p f d -> p d f"),
                                     ACT.Copy).then_inc(e_ready, 1)

            def layer1_out(t, par):
                act.wait_ge(l1_done, t + 1)
                nc.scalar.activation(p_hi[:, par, :], l1_bank[:, :], ACT.Relu).then_inc(p_ready, 1)

            def high_part(t, k, par):
                act.wait_ge(z_ready, CHUNKS * t + k + 1)
                if k == 0:
                    wait(act, l1_done, t - 1)
                nc.scalar.activation(z_hi[:, par, k, :], z[:, k, :], ACT.Copy).then_inc(z_hi_ready, 1)

            def square(t, u, step, par):
                if step == 0:
                    act.wait_ge(loaded[par], 80 * (u + 1))
                    wait(act, l1_done, t - 1)
                    wait(act, z_lo_ready, Z_OPS * t)
                dst = (z_last[:, :], z_stack[0:F, par, :], z_stack[2 * F:3 * F, par, :])[step]
                nc.scalar.activation(dst, xb[0:F, par, 0, :], ACT.Square).then_inc(squared, 1)

            def tile(t, u, par):
                act.wait_ge(x_ready, t + 1)
                for at in range(PAIRS):
                    j, g = at // HALF, at % HALF
                    act.wait_ge(a_done, PAIRS * t + at + 1)
                    wait(act, d_added, PAIRS * t + at + 1 - 2 * HALF)
                    for h in range(HG):
                        field = 2 * HG * g + h
                        last = nc.scalar.activation(scaled[:, at % (2 * HALF), h * N:(h + 1) * N],
                                                    a_bank[bank(par, at, A_BANKS)[0]][:, h, :], ACT.Copy,
                                                    scale=x_now[:, par, j, field:field + 1])
                    last.then_inc(a_scaled, 1)
                    if there(t + 2) and at in SQUARE_AT:
                        square(t + 2, u + 1, SQUARE_AT.index(at), par)
                    if there(t + 2) and at in ZH_AT:
                        high_part(t + 2, ZH_AT.index(at), par)
                    if at in IN_PLACE_AT:
                        act.wait_ge(d_done, PAIRS * t + at + 1)
                        for h in range(HG):
                            field = 2 * HG * g + HG + h
                            block_ = d_bank[bank(par, at, D_BANKS)[0]][:, h, :]
                            last = nc.scalar.activation(block_, block_, ACT.Copy,
                                                        scale=x_now[:, par, j, field:field + 1])
                        last.then_inc(in_place, 1)
                    if there(t + 1) and at == P_AT:
                        layer1_out(t + 1, 1 - par)

            def pair_of_tiles(u, b, first):
                for par in range(2):
                    tile(2 * u + par, u, par)

            turn_out(0)
            for step in range(SQUARES):
                square(0, 0, step, 0)
            for k in range(CHUNKS):
                high_part(0, k, 0)
            layer1_out(0, 0)
            for step in range(SQUARES):
                square(1, 0, step, 1)
            for k in range(CHUNKS):
                high_part(1, k, 1)
            act.wait_ge(w1_ready, 1)
            over_tiles(act, pair_of_tiles, turn_out)

            act.wait_ge(tower_in, 6 * 16)
            for half in range(2):
                act.wait_ge(rows_turned, half + 1)
                nc.scalar.activation(feat2[:, half * HALF_B:(half + 1) * HALF_B], turn_banks[half],
                                     ACT.Copy).then_inc(feat2_ready, 1)
            step = 0
            for half in range(2):
                cols = slice(half * HALF_B, (half + 1) * HALF_B)
                for c in range(H1 // P):
                    step += 1
                    act.wait_ge(tower_done, step)
                    nc.scalar.activation(h1[:, c, cols], d_bank[step % 2][:, :, :].rearrange("p a b -> p (a b)"),
                                         ACT.Relu, bias=bt1_sb[:, c:c + 1]).then_inc(tower_out, 1)
            for half in range(2):
                cols = slice(half * HALF_B, (half + 1) * HALF_B)
                for c in range(H2 // P):
                    step += 1
                    act.wait_ge(tower_done, step)
                    nc.scalar.activation(h2[:, c, cols], d_bank[step % 2][:, :, :].rearrange("p a b -> p (a b)"),
                                         ACT.Relu, bias=bt2_sb[:, c:c + 1]).then_inc(tower_out, 1)
            for half in range(2):
                cols = slice(half * HALF_B, (half + 1) * HALF_B)
                step += 1
                act.wait_ge(tower_done, step)
                nc.scalar.activation(y_sb[:, cols], d_bank[step % 2][0:1, :, :].rearrange("p a b -> p (a b)"),
                                     ACT.Copy).then_inc(tower_out, 1)

        @block.vector
        def _(dve):
            dve.wait_ge(w0_in, 48)
            most, rest = slice(0, (CHUNKS - 1) * N), slice((CHUNKS - 1) * N, CHUNKS * N)
            nc.vector.tensor_tensor(w0[:, most], w0[:, most], w0b[:, most], ALU.add)
            for q in range(3):
                rows = slice(F * q, F * (q + 1))
                last = nc.vector.tensor_tensor(w0[rows, rest], w0[rows, rest], w0b[rows, rest], ALU.add)
            last.then_inc(w0_summed, 1)
            dve.wait_ge(w0_hi_ready, 1)
            nc.vector.tensor_tensor(w0l[:, :, :].rearrange(flat), w0, w0h[:, :, :].rearrange(flat).bitcast(F32),
                                    ALU.subtract)
            nc.vector.tensor_tensor(w0_stack[2 * F:3 * F, :], w0c, w0_stack[0:F, :].bitcast(F32),
                                    ALU.subtract).then_inc(w0_ready, 1)
            nc.vector.memset(zeros[:, :], 0.0)
            for half in range(2):
                nc.vector.memset(sum1[:, half * C:(half + 1) * C], 0.0).then_inc(sum1_cleared, 1)
            dve.wait_ge(w1_hi_ready, 1)
            nc.vector.tensor_tensor(w1l[:, :, :], w1_stage, w1h[:, :, :].bitcast(F32),
                                    ALU.subtract).then_inc(w1_ready, 1)

            def copy_x(t, par):
                wait(dve, a_scaled, PAIRS * (t - 1))
                wait(dve, d_added, PAIRS * (t - 1))
                dve.wait_ge(e_ready, (t >> 3) + 1)
                nc.vector.tensor_copy(x_now[:, par, :, :].rearrange(flat),
                                      e_ring[:, bass.ds(t & (2 * TPB - 1), 1), :].rearrange(flat)
                                      ).then_inc(x_ready, 1)

            def products(t, u, k, par):
                if k == 0:
                    dve.wait_ge(loaded[par], 80 * (u + 1))
                    wait(dve, z_lo_ready, Z_OPS * t)
                    wait(dve, z_hi_ready, CHUNKS * t)
                nc.vector.tensor_tensor(z[:, k, :], xb[:, par, 0, :], xb[:, par, k + 1, :],
                                        ALU.mult).then_inc(z_ready, 1)

            def products_low(t, k, par):
                if k == 0:
                    wait(dve, l1_done, t - 1)
                if k < CHUNKS:
                    dve.wait_ge(z_hi_ready, CHUNKS * t + k + 1)
                    nc.vector.tensor_tensor(z_lo[:, par, k, :], z[:, k, :], z_hi[:, par, k, :].bitcast(F32),
                                            ALU.subtract).then_inc(z_lo_ready, 1)
                else:
                    dve.wait_ge(squared, SQUARES * (t + 1))
                    nc.vector.tensor_tensor(z_stack[F:2 * F, par, :], z_last[:, :], z_stack[0:F, par, :].bitcast(F32),
                                            ALU.subtract).then_inc(z_lo_ready, 1)

            def low_part(t, par):
                dve.wait_ge(p_ready, t + 1)
                nc.vector.scalar_tensor_tensor(out=p_lo[:, par, :], in0=l1_bank[:, :], scalar=0.0,
                                               in1=p_hi[:, par, :].bitcast(F32), op0=ALU.max,
                                               op1=ALU.subtract).then_inc(p_lo_ready, 1)

            def sum_layer1(t):
                wait(dve, sum1_added, t)
                dve.wait_ge(sum1_cleared, (t >> 3) + 1)
                new = sum1[:, bass.ds((t & TPB) * (C // TPB), C)]
                nc.vector.scalar_tensor_tensor(out=new, in0=l1_bank[:, :], scalar=0.0, in1=new,
                                               op0=ALU.max, op1=ALU.add).then_inc(sum1_added, 1)

            def fold_layer1(b, step):
                at = (b & 1) * C
                if step == 0:
                    dve.wait_ge(sum1_added, TPB * (b + 1))
                    nc.vector.tensor_tensor(fold1[:, :], sum1[:, bass.ds(at, C // 2)],
                                            sum1[:, bass.ds(at + C // 2, C // 2)], ALU.add).then_inc(cols_folded, 1)
                else:
                    dve.wait_ge(cols_folded, 2 * b + 1)
                    nc.vector.tensor_tensor(feat1[:, bass.ds(b, 1), :].rearrange(flat), fold1[:, 0:P],
                                            fold1[:, P:2 * P], ALU.add).then_inc(cols_folded, 1)
                    nc.vector.tensor_copy(sum1[:, bass.ds(at, C)], zeros[:, :]).then_inc(sum1_cleared, 1)

            def sum_layer2(t, par, first):
                dve.wait_ge(pool_summed, pool_steps(t, POOL_OPS))
                new = a_part[:, par, :, :].rearrange(flat)
                if first:
                    nc.vector.tensor_scalar(sum2[:, :], new, 0.0, None, ALU.max).then_inc(combined, 1)
                else:
                    wait(dve, combined, t)
                    nc.vector.scalar_tensor_tensor(out=sum2[:, :], in0=new, scalar=0.0, in1=sum2[:, :],
                                                   op0=ALU.max, op1=ALU.add).then_inc(combined, 1)

            def fold_layer2(b, step):
                if step == 0:
                    dve.wait_ge(combined, TPB * (b + 1))
                    nc.vector.tensor_tensor(fold2[:, :], sum2[:, 0:2 * N], sum2[:, 2 * N:4 * N],
                                            ALU.add).then_inc(rows_folded, 1)
                else:
                    dve.wait_ge(rows_folded, 2 * b + 1)
                    nc.vector.tensor_tensor(feat2_rows[:, bass.ds(b, 1), :].rearrange(flat), fold2[:, 0:N],
                                            fold2[:, N:2 * N], ALU.add).then_inc(rows_folded, 1)

            def tile(t, u, b, first, par):
                dve.wait_ge(x_ready, t + 1)
                starts = isinstance(t, int) and t == 0
                for at in range(PAIRS):
                    j, g = at // HALF, at % HALF
                    slot = at % (2 * HALF)
                    if g == 0:
                        wait(dve, pool_summed, pool_steps(t, 3 * j - 4) if j >= 2 else
                             0 if starts else pool_steps(t - 1, 3 * j + 8))
                    dve.wait_ge(d_done, PAIRS * t + at + 1)
                    dve.wait_ge(a_scaled, PAIRS * t + at + 1)
                    if at in IN_PLACE_AT:
                        dve.wait_ge(in_place, len(IN_PLACE_AT) * t + IN_PLACE_AT.index(at) + 1)
                        last = nc.vector.tensor_tensor(
                            mixed[:, slot, :], d_bank[bank(par, at, D_BANKS)[0]][:, :, :].rearrange(flat),
                            scaled[:, slot, :], ALU.add)
                    for h in range(HG if at not in IN_PLACE_AT else 0):
                        field = 2 * HG * g + HG + h
                        cols = slice(h * N, (h + 1) * N)
                        last = nc.vector.scalar_tensor_tensor(
                            out=mixed[:, slot, cols], in0=d_bank[bank(par, at, D_BANKS)[0]][:, h, :],
                            scalar=x_now[:, par, j, field:field + 1], in1=scaled[:, slot, cols],
                            op0=ALU.mult, op1=ALU.add)
                    last.then_inc(d_added, 1)
                    if there(t + 2):
                        if at in Z_AT:
                            products(t + 2, u + 1, Z_AT.index(at), par)
                        if at in ZL_AT:
                            products_low(t + 2, ZL_AT.index(at), par)
                    if there(t + 1):
                        if at == X_AT:
                            copy_x(t + 1, 1 - par)
                        if at == P_LO_AT:
                            low_part(t + 1, 1 - par)
                        if at == SUM1_AT:
                            sum_layer1(t + 1)
                    if at == SUM2_AT and not starts:
                        sum_layer2(t - 1, 1 - par, first and par == 1)
                    if first and par == 0 and not starts and at in (SUM2_AT + 1, SUM2_AT + 2):
                        fold_layer2(b - 1, at - SUM2_AT - 1)
                    if first and par == 1 and not (isinstance(b, int) and b == 0) and at in (X_AT, X_AT + 1):
                        fold_layer1(b - 1, at - X_AT)

            def pair_of_tiles(u, b, first):
                for par in range(2):
                    tile(2 * u + par, u, b, first, par)

            copy_x(0, 0)
            for k in range(CHUNKS):
                products(0, 0, k, 0)
            for k in range(Z_OPS):
                products_low(0, k, 0)
            low_part(0, 0)
            sum_layer1(0)
            for k in range(CHUNKS):
                products(1, 0, k, 1)
            for k in range(Z_OPS):
                products_low(1, k, 1)
            over_tiles(dve, pair_of_tiles, lambda b: None)
            sum_layer2(T - 1, 1, False)
            for step in range(2):
                fold_layer1(BT - 1, step)
                fold_layer2(BT - 1, step)

        @block.tensor
        def _(pe):
            def transposes(b):
                pe.wait_ge(gathered, 16 * F * (b + 1))
                wait(pe, turned_out, 2 * b)
                wait(pe, a_scaled, 0 if isinstance(b, int) and b == 0 else PAIRS * (TPB * (b - 1) + 2))
                wait(pe, sum1_added, 0 if isinstance(b, int) and b == 0 else TPB * (b - 1) + 3)
                for half, turn in enumerate(turn_banks):
                    for k in range(4):
                        f = 4 * (half * 4 + k)
                        last = nc.tensor.transpose(turn[:, k * P:(k + 1) * P],
                                                   landing[:, f:f + 4, :].rearrange("p f d -> p (f d)"),
                                                   ident[:, :])
                    last.then_inc(turned, 1)

            def layer1(t, n, par):
                k, which = n // 3, n % 3
                if n == 0:
                    wait(pe, sum1_added, t)
                if k < CHUNKS:
                    if which == 0:
                        pe.wait_ge(z_lo_ready, Z_OPS * t + k + 1)
                    nc.tensor.matmul(l1_bank[:, :], (w0h, w0l, w0h)[which][:, k, :],
                                     (z_hi, z_hi, z_lo)[which][:, par, k, :], start=n == 0, stop=False)
                else:
                    pe.wait_ge(z_lo_ready, Z_OPS * (t + 1))
                    pe.wait_ge(squared, SQUARES * (t + 1))
                    nc.tensor.matmul(l1_bank[:, :], w0_stack[:, :], z_stack[:, par, :], start=False,
                                     stop=True).then_inc(l1_done, 1)

            def group(bank_, j, h, par):
                cols = slice(j * P, (j + 1) * P)
                o = bank_[:, :, :].rearrange(flat)
                hi = w1h[:, h:h + HG, :].rearrange("p a b -> p (a b)")
                lo = w1l[:, h:h + HG, :].rearrange("p a b -> p (a b)")
                nc.tensor.matmul(o, p_hi[:, par, cols], hi, start=True, stop=False)
                nc.tensor.matmul(o, p_hi[:, par, cols], lo, start=False, stop=False)
                return nc.tensor.matmul(o, p_lo[:, par, cols], hi, start=False, stop=True)

            def tile(t, b_turned, par):
                pe.wait_ge(p_ready, t + 1)
                pe.wait_ge(p_lo_ready, t + 1)
                pe.wait_ge(turned_out, 2 * (b_turned + 1))
                for at in range(PAIRS):
                    j, g = at // HALF, at % HALF
                    which, before = bank(par, at, A_BANKS)
                    wait(pe, a_scaled, PAIRS * t + at + 1 - before)
                    group(a_bank[which], j, 2 * HG * g, par).then_inc(a_done, 1)
                    which, before = bank(par, at, D_BANKS)
                    wait(pe, d_added, PAIRS * t + at + 1 - before)
                    group(d_bank[which], j, 2 * HG * g + HG, par).then_inc(d_done, 1)
                    if there(t + 1) and at < len(L1_AT):
                        for n in range(sum(L1_AT[:at]), sum(L1_AT[:at + 1])):
                            layer1(t + 1, n, 1 - par)

            def pair_of_tiles(u, b, first):
                for par in range(2):
                    tile(2 * u + par, b if first or (isinstance(b, int) and b == BT - 1) else b + 1, par)

            pe.wait_ge(ident_made, 2)
            transposes(0)
            pe.wait_ge(turned_out, 2)
            pe.wait_ge(w0_ready, 1)
            for n in range(3 * CHUNKS + 1):
                layer1(0, n, 0)
            pe.wait_ge(w1_ready, 1)
            over_tiles(pe, pair_of_tiles, transposes)

            pe.wait_ge(rows_folded, 2 * BT)
            for half, turn in enumerate(turn_banks):
                for k in range(DG):
                    last = nc.tensor.transpose(turn[:, k * P:(k + 1) * P], feat2_rows[:, half * DG + k, :],
                                               ident[:, :])
                last.then_inc(rows_turned, 1)
            pe.wait_ge(cols_folded, 2 * BT)
            pe.wait_ge(dense_in, 16)
            pe.wait_ge(feat2_ready, 2)
            pe.wait_ge(tower_in, 6 * 16)
            step = 0

            def bank_of(step, rows):
                wait(pe, tower_out, step - 2)
                return d_bank[step % 2][0:rows, :, :].rearrange("p a b -> p (a b)")

            for half in range(2):
                cols = slice(half * HALF_B, (half + 1) * HALF_B)
                for c in range(H1 // P):
                    step += 1
                    o, n = bank_of(step, P), slice(c * P, (c + 1) * P)
                    nc.tensor.matmul(o, wt1_sb[:, 0, n], feat1_cols[:, cols], start=True, stop=False)
                    nc.tensor.matmul(o, wt1_sb[:, 1, n], feat2[:, cols], start=False, stop=False)
                    nc.tensor.matmul(o, wt1_dense[:, n], dense_sb[:, cols], start=False,
                                     stop=True).then_inc(tower_done, 1)
            for half in range(2):
                cols = slice(half * HALF_B, (half + 1) * HALF_B)
                pe.wait_ge(tower_out, (half + 1) * (H1 // P))
                for c in range(H2 // P):
                    step += 1
                    o = bank_of(step, P)
                    for k in range(H1 // P):
                        last = nc.tensor.matmul(o, wt2_sb[:, k, c * P:(c + 1) * P], h1[:, k, cols],
                                                start=k == 0, stop=k == H1 // P - 1)
                    last.then_inc(tower_done, 1)
            for half in range(2):
                cols = slice(half * HALF_B, (half + 1) * HALF_B)
                pe.wait_ge(tower_out, 2 * (H1 // P) + (half + 1) * (H2 // P))
                step += 1
                o = bank_of(step, 1)
                for k in range(H2 // P):
                    last = nc.tensor.matmul(o, wt3_sb[:, k:k + 1], h2[:, k, cols], start=k == 0,
                                            stop=k == H2 // P - 1)
                last.then_inc(tower_done, 1)


def kernel(**inputs):
    import numpy as np
    import concourse.bacc as bacc
    from concourse.bass_utils import run_bass_kernel_spmd

    own = np.arange(F)
    w0 = np.asarray(inputs["L0_rec_filter_0"])[0]
    shift = 1 + np.arange(4 * CHUNKS)
    other = (own[None, :] + shift[:, None]) % F

    def chunked(rows):
        return np.ascontiguousarray(w0[rows.ravel()].reshape(CHUNKS, P, N).transpose(1, 0, 2))

    arrays = {
        "dense_t": np.ascontiguousarray(np.asarray(inputs["dense_ctx"]).T),
        "ids": np.ascontiguousarray(inputs["ids"]),
        "w0_pairs": chunked(own[None, :] * F + other),
        "w0_swapped": chunked(other * F + own[None, :]),
        "w0_last": np.ascontiguousarray(w0[own * F + own]),
        "w1": np.ascontiguousarray(np.asarray(inputs["L0_rec_filter_1"])[0]),
        "wt1": np.ascontiguousarray(inputs["W_top1"]), "bt1": np.ascontiguousarray(inputs["b_top1"]),
        "wt2": np.ascontiguousarray(inputs["W_top2"]), "bt2": np.ascontiguousarray(inputs["b_top2"]),
        "wt3": np.ascontiguousarray(inputs["W_top3"]),
    }
    tables = {f"tbl_{f}": np.ascontiguousarray(inputs[f"tbl_{f}"]) for f in range(F)}
    nc = bacc.Bacc("TRN2", target_bir_lowering=False, num_devices=1)

    def declare(name, a):
        return nc.dram_tensor(f"in_{name}", a.shape, mybir.dt.from_np(a.dtype), kind="ExternalInput").ap()

    args = {name: declare(name, a) for name, a in arrays.items()}
    args["tables"] = [declare(name, a) for name, a in tables.items()]
    args["out"] = nc.dram_tensor("out_y", (B, 1), F32, kind="ExternalOutput").ap()
    build_cin_tower(nc, **args)
    fed = {f"in_{name}": a for name, a in {**arrays, **tables}.items()}
    r = run_bass_kernel_spmd(nc, [fed], core_ids=[0])
    return r.results[0]["out_y"]
```

```python
import concourse.bass as bass
from concourse import mybir
from contextlib import ExitStack

F32 = mybir.dt.float32
F32R = mybir.dt.float32r
I32 = mybir.dt.int32
ALU = mybir.AluOpType
ACT = mybir.ActivationFunctionType

B, F, D = 1024, 32, 32
N = 128
P = 128
BT = B // P
DG = 4
TPB = D // DG
T = BT * TPB
C = DG * P
CHUNKS = 4
HG = C // N
GROUPS = F // HG
HALF = GROUPS // 2
D_BANKS, A_BANKS = 4, 3
PAIRS = DG * HALF
Z_OPS = CHUNKS + 1
Z_AT, ZL_AT = (0, 1, 3, 4), (6, 7, 8, 9, 10)
X_AT, P_LO_AT, SUM2_AT, SUM1_AT = 5, 11, 13, 12
SQUARE_AT, ZH_AT = (0, 1, 2), (4, 5, 6, 7)
P_AT, KEEP_AT = 10, 14
IN_PLACE_AT = (2, 8, 12)
L1_AT = (0, 2, 2, 2, 2, 1, 1, 1, 1, 1)
POOL_OPS = 3 * DG + 2
AHEAD_FROM = 2
SQUARES = 3
SPLIT_HIGH_AT = ((3, 6), (0, 1, 2, 3, 4, 5, 6, 7))
SPLIT_LOW_AT, SPLIT_LOW_NEEDS = ((5, 8), (5, 8, 9)), (1, 2, 7, 8, 10)
FEATURES2_AT = 10
H1, H2, DENSE = 512, 256, 16
TOWER_STEPS = H1 // P + H2 // P + 1
HALF_B = 512


def build_cin_tower(nc, dense_t, ids, tables, w0_pairs, w0_swapped, w0_last, w1, wt1, bt1, wt2, bt2, wt3, out):
    ctx = ExitStack()
    with ctx:
        def sb(name, shape, dt=F32):
            return ctx.enter_context(nc.sbuf_tensor(name, shape, dt))

        def sem(name):
            return ctx.enter_context(nc.semaphore(name))

        x_rows = nc.dram_tensor("x_rows", (F + F // 2, T * C), F32, kind="Internal").ap()

        w1h = sb("w1h", [P, F, N], F32R)
        w1l = sb("w1l", [P, F, N], F32R)
        w0h = sb("w0h", [P, CHUNKS, N], F32R)
        w0l = sb("w0l", [P, CHUNKS, N], F32R)
        w0_stack = sb("w0_stack", [3 * F, N], F32R)
        ident = sb("ident", [P, P])
        ids_all = sb("ids_all", [P, BT, F], I32)
        ids_now = sb("ids_now", [P, F], I32)
        landing = sb("landing", [P, F, D])
        e_ring = sb("e_ring", [P, 2 * TPB, C // DG])
        x_t = sb("x_t", [P, F // 4, P])
        xb = sb("xb", [P, 2, CHUNKS + 1, C])
        z = sb("z", [P, CHUNKS, C])
        z_last = sb("z_last", [F, C])
        z_hi = sb("z_hi", [P, 2, CHUNKS, C], F32R)
        z_lo = sb("z_lo", [P, 2, CHUNKS, C], F32R)
        z_stack = sb("z_stack", [3 * F, 2, C], F32R)
        p_hi = sb("p_hi", [P, 2, C], F32R)
        p_lo = sb("p_lo", [P, 2, C], F32R)
        x_now = sb("x_now", [P, 2, DG, F])
        scaled = sb("scaled", [P, 2 * HALF, HG * N])
        mixed = sb("mixed", [P, 2 * HALF, HG * N])
        pair = sb("pair", [P, 2, HG * N])
        a_sum = sb("a_sum", [P, DG, HG * N])
        a_fold = sb("a_fold", [P, DG, 2 * N])
        a_part = sb("a_part", [P, 2, DG, N])
        sum1 = sb("sum1", [P, 2 * C])
        zeros = sb("zeros", [P, C])
        sum2 = sb("sum2", [P, DG * N])
        y_sb = sb("y_sb", [1, B])
        fold1 = sb("fold1", [P, C // 2])
        fold2 = sb("fold2", [P, DG * N // 2])
        feat1 = sb("feat1", [P, BT, P])
        feat2_rows = sb("feat2_rows", [P, BT, N])
        wt3_sb = sb("wt3_sb", [P, H2 // P])
        bt1_sb = sb("bt1_sb", [P, H1 // P])
        bt2_sb = sb("bt2_sb", [P, H2 // P])
        flat = "p a b -> p (a b)"
        w1_stage = scaled[:, :, :].rearrange(flat).rearrange("p (h n) -> p h n", n=N)
        mixed_flat = mixed[:, :, :].rearrange(flat)
        w0 = mixed_flat[:, 0:CHUNKS * N]
        w0b = mixed_flat[:, CHUNKS * N:2 * CHUNKS * N]
        w0c = mixed_flat[0:F, 2 * CHUNKS * N:2 * CHUNKS * N + N]
        h1 = scaled[:, :, :].rearrange(flat).rearrange("p (c b) -> p c b", b=B)
        h2 = mixed_flat[:, 0:H2 // P * B].rearrange("p (c b) -> p c b", b=B)
        dense_sb = xb[0:DENSE, 0, 0:B // C, :].rearrange("p k c -> p (k c)")
        wt1h, wt1l = z_hi[:, 0, 0:2, :], z_lo[:, 0, 0:2, :]
        wt2h, wt2l = (part[:, 0, 2:4, :].rearrange("p k c -> p (k c)").rearrange("p (k n) -> p k n", n=H2)
                      for part in (z_hi, z_lo))
        feat1h, feat1l = (part[:, 1, 0:2, :].rearrange("p k c -> p (k c)") for part in (z_hi, z_lo))
        feat2h, feat2l = (part[:, 1, 2:4, :].rearrange("p k c -> p (k c)") for part in (z_hi, z_lo))
        wd_stack = w0h[0:3 * F, :, :].rearrange(flat)
        dense_stack = z_stack[:, :, :].rearrange(flat)
        h1h, h1l = (part[:, :, :].rearrange(flat).rearrange("p (c b) -> p c b", b=B) for part in (w1h, w1l))
        wt1_sb = landing[:, :, :].rearrange(flat).rearrange("p (k n) -> p k n", n=H1)
        wt1_dense = x_t[0:DENSE, :, :].rearrange(flat)[:, 0:H1]
        wt2_sb = e_ring[:, 0:TPB, :].rearrange(flat).rearrange("p (k n) -> p k n", n=H2)
        feat1_cols = feat1[:, :, :].rearrange(flat)

        d_bank = [ctx.enter_context(nc.psum_tensor(f"d_bank{i}", [P, HG, N], F32)) for i in range(D_BANKS)]
        a_bank = [ctx.enter_context(nc.psum_tensor(f"a_bank{i}", [P, HG, N], F32)) for i in range(A_BANKS)]
        l1_bank = ctx.enter_context(nc.psum_tensor("l1_bank", [P, C], F32))
        turn_banks = (a_bank[2][:, :, :].rearrange(flat), l1_bank[:, :])

        ids_in = sem("ids_in")
        w0_in = sem("w0_in")
        w1_in = sem("w1_in")
        tower_in = sem("tower_in")
        dense_in = sem("dense_in")
        gathered = sem("gathered")
        x_rows_out = sem("x_rows_out")
        loaded = [sem("loaded0"), sem("loaded1")]
        y_out = sem("y_out")
        ident_made = sem("ident_made")
        ids_moved = sem("ids_moved")
        w0_summed = sem("w0_summed")
        w0_hi_ready = sem("w0_hi_ready")
        w0_ready = sem("w0_ready")
        w1_hi_ready = sem("w1_hi_ready")
        w1_ready = sem("w1_ready")
        turned = sem("turned")
        turned_out = sem("turned_out")
        e_ready = sem("e_ready")
        x_ready = sem("x_ready")
        z_ready = sem("z_ready")
        z_hi_ready = sem("z_hi_ready")
        squared = sem("squared")
        z_lo_ready = sem("z_lo_ready")
        l1_done = sem("l1_done")
        p_ready = sem("p_ready")
        p_lo_ready = sem("p_lo_ready")
        d_done = sem("d_done")
        a_done = sem("a_done")
        in_place = sem("in_place")
        sum1_cleared = sem("sum1_cleared")
        sum1_added = sem("sum1_added")
        d_added = sem("d_added")
        a_scaled = sem("a_scaled")
        pool_summed = sem("pool_summed")
        combined = sem("combined")
        rows_folded = sem("rows_folded")
        cols_folded = sem("cols_folded")
        rows_turned = sem("rows_turned")
        tower_hi = sem("tower_hi")
        tower_lo = sem("tower_lo")
        feat_hi = sem("feat_hi")
        feat_lo = sem("feat_lo")
        h1_lo_ready = sem("h1_lo_ready")
        tower_done = sem("tower_done")
        tower_out = sem("tower_out")

        def there(t):
            return not isinstance(t, int) or t < T

        def wait(eng, semaphore, value):
            if not isinstance(value, int) or value > 0:
                eng.wait_ge(semaphore, value)

        def bank(par, at, banks):
            n = PAIRS * par + at
            return n % banks, next(d for d in range(1, 2 * PAIRS) if (n - d) % (2 * PAIRS) % banks == n % banks)

        def pool_steps(t, k):
            return POOL_OPS * t + k

        def over_tiles(eng, pair_of_tiles, between, peeled=1):
            pairs = TPB // 2

            pair_of_tiles(0, 0, True)
            between(1)
            with eng.Fori(1, pairs) as i:
                pair_of_tiles(i, 0, False)
            with eng.Fori(1, BT - 1) as b:
                pair_of_tiles(b * pairs, b, True)
                between(b + 1)
                with eng.Fori(1, pairs) as i:
                    pair_of_tiles(b * pairs + i, b, False)
            pair_of_tiles((BT - 1) * pairs, BT - 1, True)
            with eng.Fori((BT - 1) * pairs + 1, BT * pairs - peeled) as u:
                pair_of_tiles(u, BT - 1, False)
            for u in range(BT * pairs - peeled, BT * pairs):
                pair_of_tiles(u, BT - 1, False)

        block = ctx.enter_context(nc.Block())

        @block.sync
        def _(sp):
            sp.dma_start(ids_all[:, :, :], ids.rearrange("(t p) f -> p t f", p=P)).then_inc(ids_in, 16)
            sp.dma_start(w0, w0_pairs.rearrange("p k n -> p (k n)")).then_inc(w0_in, 16)
            sp.dma_start(w0b, w0_swapped.rearrange("p k n -> p (k n)")).then_inc(w0_in, 16)
            sp.dma_start(w0c, w0_last).then_inc(w0_in, 16)
            sp.dma_start(w1_stage, w1.rearrange("(h m) n -> m h n", m=N)).then_inc(w1_in, 16)
            with nc.allow_non_contiguous_dma(reason="a few hundred biases and last weights"):
                sp.dma_start(wt3_sb[:, :], wt3.rearrange("(k p) n -> p (k n)", p=P)).then_inc(tower_in, 16)
                sp.dma_start(bt1_sb[:, :], bt1.rearrange("(k p) -> p k", p=P)).then_inc(tower_in, 16)
                sp.dma_start(bt2_sb[:, :], bt2.rearrange("(k p) -> p k", p=P)).then_inc(tower_in, 16)

            def write_x_rows(b):
                sp.wait_ge(turned_out, 2 * b + 2)
                for q in range(4):
                    for row, fields in ((0, F), (F, F // 2)):
                        dst = x_rows[row:row + fields, bass.ds(b * (TPB * C), TPB * C)].rearrange(
                            "(g q) (d b) -> q d g b", q=4, d=D)[q]
                        sp.dma_start(dst, x_t[D * q:D * (q + 1), 0:fields // 4, :]).then_inc(x_rows_out, 16)

            def rolls(first, copies, rows_apart, t):
                cols = x_rows[first:first + F, bass.ds(t * C, C)]
                whole = cols.ap if isinstance(cols.ap, list) else list(cols.ap)
                row, col = list(whole[0]), list(whole[1])
                return bass.AP(cols.tensor, cols.offset, [[rows_apart * row[0], copies], row, col])

            def load(t, par):
                wait(sp, z_lo_ready, Z_OPS * (t - 1))
                sp.wait_ge(x_rows_out, 128 * ((t >> 3) + 1))
                sp.dma_start(xb[:, par, 0, :], rolls(0, 4, 0, t)).then_inc(loaded[par], 16)
                for k in range(CHUNKS):
                    sp.dma_start(xb[:, par, k + 1, :], rolls(4 * k + 1, 4, 1, t)).then_inc(loaded[par], 16)

            def pair_of_tiles(u, b, first):
                for par in range(2):
                    if there(2 * u + par + 4):
                        load(2 * u + par + 4, par)

            write_x_rows(0)
            for t in range(4):
                load(t, t % 2)
            over_tiles(sp, pair_of_tiles, write_x_rows, peeled=2)
            sp.wait_ge(x_ready, T - TPB)
            sp.wait_ge(e_ready, BT)
            sp.wait_ge(turned, 2 * BT)
            sp.wait_ge(x_rows_out, 128 * BT)
            sp.dma_start(wt1_sb[:, :, :], wt1[0:2 * P, :].rearrange("(k p) n -> p k n", p=P)).then_inc(tower_in, 16)
            sp.dma_start(wt1_dense[:, :], wt1[2 * P:2 * P + DENSE, :]).then_inc(tower_in, 16)
            sp.dma_start(wt2_sb[:, :, :], wt2.rearrange("(k p) n -> p k n", p=P)).then_inc(tower_in, 16)
            sp.wait_ge(z_lo_ready, Z_OPS * (T - 1))
            sp.dma_start(dense_sb, dense_t).then_inc(dense_in, 16)
            sp.wait_ge(tower_out, 2 * (H1 // P + H2 // P + 1))
            sp.dma_start(out.rearrange("b n -> n b"), y_sb[:, :]).then_inc(y_out, 16)
            sp.wait_ge(y_out, 16)

        @block.gpsimd
        def _(pool):
            nc.gpsimd.memset(ident[:, :], 0.0).then_inc(ident_made, 1)
            pool.wait_ge(ident_made, 1)
            nc.gpsimd.affine_select(out=ident[:, :], in_=ident[:, :], compare_op=ALU.not_equal, fill=1.0,
                                    base=0, pattern=[[-1, P]], channel_multiplier=1).then_inc(ident_made, 1)
            pool.wait_ge(ids_in, 16)

            def move_ids(b):
                wait(pool, gathered, 16 * F * b)
                nc.gpsimd.tensor_copy(ids_now[:, :], ids_all[:, bass.ds(b, 1), :].rearrange(
                    "p a f -> p (a f)")).then_inc(ids_moved, 1)

            def gather(b, fields):
                for f in fields:
                    nc.gpsimd.indirect_dma_start(landing[:, f, :], None, tables[f], bass.IndirectOffsetOnAxis(
                        ap=ids_now[:, f:f + 1], axis=0)).then_inc(gathered, 16)

            def free_landing(b):
                wait(pool, e_ready, b)
                wait(pool, turned, 2 * b)

            def add(out_, in0, in1):
                nc.gpsimd.tensor_tensor(out_, in0, in1, ALU.add).then_inc(pool_summed, 1)

            def tile(t, b, k, ahead, late):
                par = k % 2
                for j in range(DG):
                    if ahead and (k, j) == (AHEAD_FROM, 2):
                        pool.wait_ge(ids_moved, b + 3)
                    ring = HALF * (j % 2)
                    at = 3 * j
                    for half in range(2):
                        pool.wait_ge(d_added, PAIRS * t + HALF * j + 2 * half + 2)
                        if half == 0:
                            wait(pool, pool_summed, pool_steps(t, at))
                        add(pair[:, half, :], mixed[:, ring + 2 * half, :], mixed[:, ring + 2 * half + 1, :])
                    pool.wait_ge(pool_summed, pool_steps(t, at + 2))
                    add(a_sum[:, j, :], pair[:, 0, :], pair[:, 1, :])
                    if ahead and (k, j) == (AHEAD_FROM, 1):
                        free_landing(b + 2)
                        move_ids(b + 2)
                    if k >= AHEAD_FROM and ahead:
                        gather(b + 2, at_slot.get((k, j), ()))
                    if k == 0 and late:
                        gather(b + 1, at_slot.get((k, j), ()))
                pool.wait_ge(pool_summed, pool_steps(t, 3 * DG))
                add(a_fold[:, :, :], a_sum[:, :, 0:2 * N], a_sum[:, :, 2 * N:4 * N])
                pool.wait_ge(pool_summed, pool_steps(t, 3 * DG + 1))
                wait(pool, combined, t - 1)
                add(a_part[:, par, :, :], a_fold[:, :, 0:N], a_fold[:, :, N:2 * N])

            move_ids(0)
            pool.wait_ge(ids_moved, 1)
            gather(0, range(F))
            free_landing(1)
            move_ids(1)
            pool.wait_ge(ids_moved, 2)
            gather(1, range(F))

            slots = [(k, j) for k in (*range(AHEAD_FROM, TPB), 0) for j in range(DG)][2:]
            at_slot = {slot: range(F * n // len(slots), F * (n + 1) // len(slots)) for n, slot in enumerate(slots)}

            def b_tile(b, ahead, late):
                for k in range(TPB):
                    tile(b * TPB + k, b, k, ahead, late)

            b_tile(0, True, False)
            with pool.Fori(1, BT - 2) as b:
                b_tile(b, True, True)
            b_tile(BT - 2, False, True)
            b_tile(BT - 1, False, False)

        @block.scalar
        def _(act):
            act.wait_ge(w0_summed, 1)
            nc.scalar.activation(w0h[:, :, :].rearrange(flat), w0, ACT.Copy)
            for q in range(2):
                last = nc.scalar.activation(w0_stack[F * q:F * (q + 1), :], w0c, ACT.Copy)
            last.then_inc(w0_hi_ready, 1)
            act.wait_ge(w1_in, 16)
            nc.scalar.activation(w1h[:, :, :], w1_stage, ACT.Copy).then_inc(w1_hi_ready, 1)

            def turn_out(b):
                wait(act, x_rows_out, 128 * b)
                for half, turn in enumerate(turn_banks):
                    act.wait_ge(turned, 2 * b + half + 1)
                    nc.scalar.activation(x_t[:, half * DG:(half + 1) * DG, :].rearrange("p g b -> p (g b)"),
                                         turn, ACT.Copy).then_inc(turned_out, 1)

            def keep_scalars(b):
                act.wait_ge(gathered, 16 * F * (b + 1))
                ring = e_ring[:, bass.ds((b & 1) * TPB, TPB), :].rearrange("p g (j f) -> p (g j) f", f=F)
                nc.scalar.activation(ring, landing[:, :, :].rearrange("p f d -> p d f"),
                                     ACT.Copy).then_inc(e_ready, 1)

            def layer1_out(t, par):
                act.wait_ge(l1_done, t + 1)
                nc.scalar.activation(p_hi[:, par, :], l1_bank[:, :], ACT.Relu).then_inc(p_ready, 1)

            def high_part(t, k, par):
                act.wait_ge(z_ready, CHUNKS * t + k + 1)
                if k == 0:
                    wait(act, l1_done, t - 1)
                nc.scalar.activation(z_hi[:, par, k, :], z[:, k, :], ACT.Copy).then_inc(z_hi_ready, 1)

            def square(t, u, step, par):
                if step == 0:
                    act.wait_ge(loaded[par], 80 * (u + 1))
                    wait(act, l1_done, t - 1)
                    wait(act, z_lo_ready, Z_OPS * t)
                dst = (z_last[:, :], z_stack[0:F, par, :], z_stack[2 * F:3 * F, par, :])[step]
                nc.scalar.activation(dst, xb[0:F, par, 0, :], ACT.Square).then_inc(squared, 1)

            def tile(t, u, b, first, par):
                act.wait_ge(x_ready, t + 1)
                for at in range(PAIRS):
                    j, g = at // HALF, at % HALF
                    act.wait_ge(a_done, PAIRS * t + at + 1)
                    wait(act, d_added, PAIRS * t + at + 1 - 2 * HALF)
                    for h in range(HG):
                        field = 2 * HG * g + h
                        last = nc.scalar.activation(scaled[:, at % (2 * HALF), h * N:(h + 1) * N],
                                                    a_bank[bank(par, at, A_BANKS)[0]][:, h, :], ACT.Copy,
                                                    scale=x_now[:, par, j, field:field + 1])
                    last.then_inc(a_scaled, 1)
                    if there(t + 2) and at in SQUARE_AT:
                        square(t + 2, u + 1, SQUARE_AT.index(at), par)
                    if there(t + 2) and at in ZH_AT:
                        high_part(t + 2, ZH_AT.index(at), par)
                    if at in IN_PLACE_AT:
                        act.wait_ge(d_done, PAIRS * t + at + 1)
                        for h in range(HG):
                            field = 2 * HG * g + HG + h
                            block_ = d_bank[bank(par, at, D_BANKS)[0]][:, h, :]
                            last = nc.scalar.activation(block_, block_, ACT.Copy,
                                                        scale=x_now[:, par, j, field:field + 1])
                        last.then_inc(in_place, 1)
                    if there(t + 1) and at == P_AT:
                        layer1_out(t + 1, 1 - par)
                    if not there(t + 2) and at in SPLIT_HIGH_AT[par]:
                        split_high(par * len(SPLIT_HIGH_AT[0]) + SPLIT_HIGH_AT[par].index(at))
                    if not there(t + 1) and at == FEATURES2_AT - 1:
                        features2_high(0)
                    if first and par == 1 and at == KEEP_AT and not (isinstance(b, int) and b == BT - 1):
                        keep_scalars(b + 1)

            def pair_of_tiles(u, b, first):
                for par in range(2):
                    tile(2 * u + par, u, b, first, par)

            def split_high(k):
                if k == 0:
                    act.wait_ge(tower_in, 6 * 16)
                    act.wait_ge(l1_done, T - 1)
                if k == 2:
                    act.wait_ge(dense_in, 16)
                    act.wait_ge(l1_done, T)
                    act.wait_ge(cols_folded, BT)
                if k > 2:
                    act.wait_ge(tower_hi, k)
                dst, src = (
                    (wt1h, wt1_sb[:, :, :]),
                    (wt2h, wt2_sb[:, :, :]),
                    (z_stack[:, 0, :], zeros[0:3 * F, :]),
                    (z_stack[:, 1, :], zeros[0:3 * F, :]),
                    (wd_stack[:, :], zeros[0:3 * F, :]),
                    (wd_stack[0:DENSE, :], wt1_dense),
                    (wd_stack[F:F + DENSE, :], wt1_dense),
                    (dense_stack[0:DENSE, :], dense_sb),
                    (dense_stack[2 * F:2 * F + DENSE, :], dense_sb),
                    (feat1h[:, 0:HALF_B], feat1_cols[:, 0:HALF_B]))[k]
                nc.scalar.activation(dst, src, ACT.Copy).then_inc(tower_hi, 1)

            def features2_high(half):
                act.wait_ge(rows_turned, half + 1)
                nc.scalar.activation(feat2h[:, half * HALF_B:(half + 1) * HALF_B], l1_bank[:, :],
                                     ACT.Copy).then_inc(feat_hi, 1)

            turn_out(0)
            keep_scalars(0)
            for k in range(CHUNKS):
                high_part(0, k, 0)
            for step in range(SQUARES):
                square(0, 0, step, 0)
            layer1_out(0, 0)
            for step in range(SQUARES):
                square(1, 0, step, 1)
            for k in range(CHUNKS):
                high_part(1, k, 1)
            act.wait_ge(w1_ready, 1)
            over_tiles(act, pair_of_tiles, turn_out)

            act.wait_ge(tower_in, 6 * 16)
            act.wait_ge(d_added, PAIRS * T)
            step = 0
            for half in range(2):
                cols = slice(half * HALF_B, (half + 1) * HALF_B)
                if half == 1:
                    act.wait_ge(cols_folded, 2 * BT)
                    nc.scalar.activation(feat1h[:, cols], feat1_cols[:, cols], ACT.Copy).then_inc(feat_hi, 1)
                    features2_high(1)
                for c in range(H1 // P):
                    step += 1
                    act.wait_ge(tower_done, step)
                    product = a_bank[step % 2][:, :, :].rearrange(flat)
                    nc.scalar.activation(h1h[:, c, cols], product, ACT.Relu, bias=bt1_sb[:, c:c + 1])
                    nc.scalar.activation(h1[:, c, cols], product, ACT.Relu,
                                         bias=bt1_sb[:, c:c + 1]).then_inc(tower_out, 1)
                act.wait_ge(pool_summed, pool_steps(T - 1, 3 * DG))
                for c in range(H2 // P):
                    step += 1
                    act.wait_ge(tower_done, step)
                    nc.scalar.activation(h2[:, c, cols], a_bank[step % 2][:, :, :].rearrange(flat),
                                         ACT.Relu, bias=bt2_sb[:, c:c + 1]).then_inc(tower_out, 1)
                step += 1
                act.wait_ge(tower_done, step)
                nc.scalar.activation(y_sb[:, cols], a_bank[step % 2][0:1, :, :].rearrange(flat),
                                     ACT.Copy).then_inc(tower_out, 1)

        @block.vector
        def _(dve):
            dve.wait_ge(w0_in, 48)
            most, rest = slice(0, (CHUNKS - 1) * N), slice((CHUNKS - 1) * N, CHUNKS * N)
            nc.vector.tensor_tensor(w0[:, most], w0[:, most], w0b[:, most], ALU.add)
            for q in range(3):
                rows = slice(F * q, F * (q + 1))
                last = nc.vector.tensor_tensor(w0[rows, rest], w0[rows, rest], w0b[rows, rest], ALU.add)
            last.then_inc(w0_summed, 1)
            dve.wait_ge(w0_hi_ready, 1)
            nc.vector.tensor_tensor(w0l[:, :, :].rearrange(flat), w0, w0h[:, :, :].rearrange(flat).bitcast(F32),
                                    ALU.subtract)
            nc.vector.tensor_tensor(w0_stack[2 * F:3 * F, :], w0c, w0_stack[0:F, :].bitcast(F32),
                                    ALU.subtract).then_inc(w0_ready, 1)
            nc.vector.memset(zeros[:, :], 0.0)
            for half in range(2):
                nc.vector.memset(sum1[:, half * C:(half + 1) * C], 0.0).then_inc(sum1_cleared, 1)
            dve.wait_ge(w1_hi_ready, 1)
            nc.vector.tensor_tensor(w1l[:, :, :], w1_stage, w1h[:, :, :].bitcast(F32),
                                    ALU.subtract).then_inc(w1_ready, 1)

            def copy_x(t, par):
                wait(dve, a_scaled, PAIRS * (t - 1))
                wait(dve, d_added, PAIRS * (t - 1))
                dve.wait_ge(e_ready, (t >> 3) + 1)
                nc.vector.tensor_copy(x_now[:, par, :, :].rearrange(flat),
                                      e_ring[:, bass.ds(t & (2 * TPB - 1), 1), :].rearrange(flat)
                                      ).then_inc(x_ready, 1)

            def products(t, u, k, par):
                if k == 0:
                    dve.wait_ge(loaded[par], 80 * (u + 1))
                    wait(dve, z_lo_ready, Z_OPS * t)
                    wait(dve, z_hi_ready, CHUNKS * t)
                nc.vector.tensor_tensor(z[:, k, :], xb[:, par, 0, :], xb[:, par, k + 1, :],
                                        ALU.mult).then_inc(z_ready, 1)

            def products_low(t, k, par):
                if k == 0:
                    wait(dve, l1_done, t - 1)
                if k < CHUNKS:
                    dve.wait_ge(z_hi_ready, CHUNKS * t + k + 1)
                    nc.vector.tensor_tensor(z_lo[:, par, k, :], z[:, k, :], z_hi[:, par, k, :].bitcast(F32),
                                            ALU.subtract).then_inc(z_lo_ready, 1)
                else:
                    dve.wait_ge(squared, SQUARES * (t + 1))
                    nc.vector.tensor_tensor(z_stack[F:2 * F, par, :], z_last[:, :], z_stack[0:F, par, :].bitcast(F32),
                                            ALU.subtract).then_inc(z_lo_ready, 1)

            def low_part(t, par):
                dve.wait_ge(p_ready, t + 1)
                nc.vector.scalar_tensor_tensor(out=p_lo[:, par, :], in0=l1_bank[:, :], scalar=0.0,
                                               in1=p_hi[:, par, :].bitcast(F32), op0=ALU.max,
                                               op1=ALU.subtract).then_inc(p_lo_ready, 1)

            def sum_layer1(t):
                wait(dve, sum1_added, t)
                dve.wait_ge(sum1_cleared, (t >> 3) + 1)
                new = sum1[:, bass.ds((t & TPB) * (C // TPB), C)]
                nc.vector.scalar_tensor_tensor(out=new, in0=l1_bank[:, :], scalar=0.0, in1=new,
                                               op0=ALU.max, op1=ALU.add).then_inc(sum1_added, 1)

            def fold_layer1(b, step):
                at = (b & 1) * C
                if step == 0:
                    dve.wait_ge(sum1_added, TPB * (b + 1))
                    nc.vector.tensor_tensor(fold1[:, :], sum1[:, bass.ds(at, C // 2)],
                                            sum1[:, bass.ds(at + C // 2, C // 2)], ALU.add).then_inc(cols_folded, 1)
                else:
                    dve.wait_ge(cols_folded, 2 * b + 1)
                    nc.vector.tensor_tensor(feat1[:, bass.ds(b, 1), :].rearrange(flat), fold1[:, 0:P],
                                            fold1[:, P:2 * P], ALU.add).then_inc(cols_folded, 1)
                    nc.vector.tensor_copy(sum1[:, bass.ds(at, C)], zeros[:, :]).then_inc(sum1_cleared, 1)

            def sum_layer2(t, par, first):
                dve.wait_ge(pool_summed, pool_steps(t, POOL_OPS))
                new = a_part[:, par, :, :].rearrange(flat)
                if first:
                    nc.vector.tensor_scalar(sum2[:, :], new, 0.0, None, ALU.max).then_inc(combined, 1)
                else:
                    wait(dve, combined, t)
                    nc.vector.scalar_tensor_tensor(out=sum2[:, :], in0=new, scalar=0.0, in1=sum2[:, :],
                                                   op0=ALU.max, op1=ALU.add).then_inc(combined, 1)

            def fold_layer2(b, step):
                if step == 0:
                    dve.wait_ge(combined, TPB * (b + 1))
                    nc.vector.tensor_tensor(fold2[:, :], sum2[:, 0:2 * N], sum2[:, 2 * N:4 * N],
                                            ALU.add).then_inc(rows_folded, 1)
                else:
                    dve.wait_ge(rows_folded, 2 * b + 1)
                    nc.vector.tensor_tensor(feat2_rows[:, bass.ds(b, 1), :].rearrange(flat), fold2[:, 0:N],
                                            fold2[:, N:2 * N], ALU.add).then_inc(rows_folded, 1)

            def tile(t, u, b, first, par):
                dve.wait_ge(x_ready, t + 1)
                starts = isinstance(t, int) and t == 0
                for at in range(PAIRS):
                    j, g = at // HALF, at % HALF
                    slot = at % (2 * HALF)
                    if g == 0:
                        wait(dve, pool_summed, pool_steps(t, 3 * j - 4) if j >= 2 else
                             0 if starts else pool_steps(t - 1, 3 * j + 8))
                    dve.wait_ge(d_done, PAIRS * t + at + 1)
                    dve.wait_ge(a_scaled, PAIRS * t + at + 1)
                    if at in IN_PLACE_AT:
                        dve.wait_ge(in_place, len(IN_PLACE_AT) * t + IN_PLACE_AT.index(at) + 1)
                        last = nc.vector.tensor_tensor(
                            mixed[:, slot, :], d_bank[bank(par, at, D_BANKS)[0]][:, :, :].rearrange(flat),
                            scaled[:, slot, :], ALU.add)
                    for h in range(HG if at not in IN_PLACE_AT else 0):
                        field = 2 * HG * g + HG + h
                        cols = slice(h * N, (h + 1) * N)
                        last = nc.vector.scalar_tensor_tensor(
                            out=mixed[:, slot, cols], in0=d_bank[bank(par, at, D_BANKS)[0]][:, h, :],
                            scalar=x_now[:, par, j, field:field + 1], in1=scaled[:, slot, cols],
                            op0=ALU.mult, op1=ALU.add)
                    last.then_inc(d_added, 1)
                    if there(t + 2):
                        if at in Z_AT:
                            products(t + 2, u + 1, Z_AT.index(at), par)
                        if at in ZL_AT:
                            products_low(t + 2, ZL_AT.index(at), par)
                    if there(t + 1):
                        if at == X_AT:
                            copy_x(t + 1, 1 - par)
                        if at == P_LO_AT:
                            low_part(t + 1, 1 - par)
                        if at == SUM1_AT:
                            sum_layer1(t + 1)
                    if not there(t + 2) and at in SPLIT_LOW_AT[par]:
                        split_low(par * len(SPLIT_LOW_AT[0]) + SPLIT_LOW_AT[par].index(at))
                    if not there(t + 1) and at == FEATURES2_AT:
                        features_low(0, 2)
                    if at == SUM2_AT and not starts:
                        sum_layer2(t - 1, 1 - par, first and par == 1)
                    if first and par == 0 and not starts and at in (SUM2_AT + 1, SUM2_AT + 2):
                        fold_layer2(b - 1, at - SUM2_AT - 1)
                    if first and par == 1 and not (isinstance(b, int) and b == 0) and at in (X_AT, X_AT + 1):
                        fold_layer1(b - 1, at - X_AT)

            def split_low(k):
                dve.wait_ge(tower_hi, SPLIT_LOW_NEEDS[k])
                dst, full, high = (
                    (wt1l, wt1_sb[:, :, :], wt1h),
                    (wt2l, wt2_sb[:, :, :], wt2h),
                    (wd_stack[2 * F:2 * F + DENSE, :], wt1_dense, wd_stack[0:DENSE, :]),
                    (dense_stack[F:F + DENSE, :], dense_sb, dense_stack[0:DENSE, :]),
                    (feat1l[:, 0:HALF_B], feat1_cols[:, 0:HALF_B], feat1h[:, 0:HALF_B]))[k]
                nc.vector.tensor_tensor(dst, full, high.bitcast(F32), ALU.subtract).then_inc(tower_lo, 1)

            def features_low(half, layer):
                cols = slice(half * HALF_B, (half + 1) * HALF_B)
                dve.wait_ge(feat_hi, 1 if half == 0 else 1 + layer)
                dst, full, high = ((feat1l[:, cols], feat1_cols[:, cols], feat1h[:, cols]) if layer == 1 else
                                   (feat2l[:, cols], l1_bank[:, :], feat2h[:, cols]))
                nc.vector.tensor_tensor(dst, full, high.bitcast(F32), ALU.subtract).then_inc(feat_lo, 1)

            def tower_low(half):
                cols = slice(half * HALF_B, (half + 1) * HALF_B)
                for c in range(H1 // P):
                    dve.wait_ge(tower_out, TOWER_STEPS * half + c + 1)
                    nc.vector.tensor_tensor(h1l[:, c, cols], h1[:, c, cols], h1h[:, c, cols].bitcast(F32),
                                            ALU.subtract).then_inc(h1_lo_ready, 1)

            def pair_of_tiles(u, b, first):
                for par in range(2):
                    tile(2 * u + par, u, b, first, par)

            copy_x(0, 0)
            for k in range(CHUNKS + 2):
                if k < CHUNKS:
                    products(0, 0, k, 0)
                if k > 0:
                    products_low(0, k - 1, 0)
            for k in range(CHUNKS):
                products(1, 0, k, 1)
            low_part(0, 0)
            sum_layer1(0)
            for k in range(Z_OPS):
                products_low(1, k, 1)
            over_tiles(dve, pair_of_tiles, lambda b: None)
            tower_low(0)
            sum_layer2(T - 1, 1, False)
            for step in range(2):
                fold_layer1(BT - 1, step)
                fold_layer2(BT - 1, step)
            features_low(1, 1)
            features_low(1, 2)
            tower_low(1)

        @block.tensor
        def _(pe):
            def transposes(b):
                pe.wait_ge(gathered, 16 * F * (b + 1))
                starts = isinstance(b, int) and b == 0
                for half, turn in enumerate(turn_banks):
                    if half == 0 and not starts:
                        pe.wait_ge(a_scaled, PAIRS * (TPB * (b - 1) + 2) - 2)
                    if half == 1 and not starts:
                        pe.wait_ge(sum1_added, TPB * (b - 1) + 3)
                    for k in range(4):
                        f = 4 * (half * 4 + k)
                        last = nc.tensor.transpose(turn[:, k * P:(k + 1) * P],
                                                   landing[:, f:f + 4, :].rearrange("p f d -> p (f d)"),
                                                   ident[:, :])
                    last.then_inc(turned, 1)

            def layer1(t, n, par, b_turned):
                k, which = n // 3, n % 3
                if n == 0:
                    pe.wait_ge(turned_out, 2 * (b_turned + 1))
                    wait(pe, sum1_added, t)
                if k < CHUNKS:
                    if which == 0:
                        pe.wait_ge(z_lo_ready, Z_OPS * t + k + 1)
                    nc.tensor.matmul(l1_bank[:, :], (w0h, w0l, w0h)[which][:, k, :],
                                     (z_hi, z_hi, z_lo)[which][:, par, k, :], start=n == 0, stop=False)
                else:
                    pe.wait_ge(z_lo_ready, Z_OPS * (t + 1))
                    pe.wait_ge(squared, SQUARES * (t + 1))
                    nc.tensor.matmul(l1_bank[:, :], w0_stack[:, :], z_stack[:, par, :], start=False,
                                     stop=True).then_inc(l1_done, 1)

            def group(bank_, j, h, par):
                cols = slice(j * P, (j + 1) * P)
                o = bank_[:, :, :].rearrange(flat)
                hi = w1h[:, h:h + HG, :].rearrange("p a b -> p (a b)")
                lo = w1l[:, h:h + HG, :].rearrange("p a b -> p (a b)")
                nc.tensor.matmul(o, p_hi[:, par, cols], hi, start=True, stop=False)
                nc.tensor.matmul(o, p_hi[:, par, cols], lo, start=False, stop=False)
                return nc.tensor.matmul(o, p_lo[:, par, cols], hi, start=False, stop=True)

            def turn_features(half):
                pe.wait_ge(rows_folded, (half + 1) * BT)
                wait(pe, feat_lo, half)
                for k in range(DG):
                    last = nc.tensor.transpose(l1_bank[:, k * P:(k + 1) * P], feat2_rows[:, half * DG + k, :],
                                               ident[:, :])
                last.then_inc(rows_turned, 1)

            def tile(t, b_turned, par):
                pe.wait_ge(p_ready, t + 1)
                pe.wait_ge(p_lo_ready, t + 1)
                for at in range(PAIRS):
                    j, g = at // HALF, at % HALF
                    which, before = bank(par, at, A_BANKS)
                    wait(pe, a_scaled, PAIRS * t + at + 1 - before)
                    if par == 0 and at == 2:
                        pe.wait_ge(turned_out, 2 * b_turned + 1)
                    group(a_bank[which], j, 2 * HG * g, par).then_inc(a_done, 1)
                    which, before = bank(par, at, D_BANKS)
                    wait(pe, d_added, PAIRS * t + at + 1 - before)
                    group(d_bank[which], j, 2 * HG * g + HG, par).then_inc(d_done, 1)
                    if not there(t + 1) and at == 1:
                        pe.wait_ge(sum1_added, T)
                        turn_features(0)
                    if there(t + 1) and at < len(L1_AT):
                        for n in range(sum(L1_AT[:at]), sum(L1_AT[:at + 1])):
                            layer1(t + 1, n, 1 - par, b_turned)

            def pair_of_tiles(u, b, first):
                for par in range(2):
                    tile(2 * u + par, b if first or (isinstance(b, int) and b == BT - 1) else b + 1, par)

            pe.wait_ge(ident_made, 2)
            transposes(0)
            pe.wait_ge(turned_out, 2)
            pe.wait_ge(w0_ready, 1)
            for n in range(3 * CHUNKS + 1):
                layer1(0, n, 0, 0)
            pe.wait_ge(w1_ready, 1)
            over_tiles(pe, pair_of_tiles, transposes)

            pe.wait_ge(a_scaled, PAIRS * T)
            step = 0

            def bank_of(step, rows):
                wait(pe, tower_out, step - 2)
                return a_bank[step % 2][0:rows, :, :].rearrange("p a b -> p (a b)")

            for half in range(2):
                cols = slice(half * HALF_B, (half + 1) * HALF_B)
                before = step
                if half == 1:
                    turn_features(1)
                pe.wait_ge(tower_lo, len(SPLIT_LOW_NEEDS))
                for c in range(H1 // P):
                    step += 1
                    o, n = bank_of(step, P), slice(c * P, (c + 1) * P)
                    nc.tensor.matmul(o, wd_stack[:, n], dense_stack[:, cols], start=True, stop=False)
                    wait(pe, feat_lo, 2 * half)
                    for w, feat in ((wt1h, feat1h), (wt1l, feat1h), (wt1h, feat1l)):
                        nc.tensor.matmul(o, w[:, 0, n], feat[:, cols], start=False, stop=False)
                    pe.wait_ge(feat_lo, 2 * half + 1)
                    for part, (w, feat) in enumerate(((wt1h, feat2h), (wt1l, feat2h), (wt1h, feat2l))):
                        last = nc.tensor.matmul(o, w[:, 1, n], feat[:, cols], start=False, stop=part == 2)
                    last.then_inc(tower_done, 1)
                for c in range(H2 // P):
                    step += 1
                    o, n = bank_of(step, P), slice(c * P, (c + 1) * P)
                    for k in range(H1 // P):
                        pe.wait_ge(h1_lo_ready, half * (H1 // P) + k + 1)
                        for part, (w, h) in enumerate(((wt2h, h1h), (wt2l, h1h), (wt2h, h1l))):
                            last = nc.tensor.matmul(o, w[:, k, n], h[:, k, cols], start=k == 0 and part == 0,
                                                    stop=k == H1 // P - 1 and part == 2)
                    last.then_inc(tower_done, 1)
                pe.wait_ge(tower_out, before + H1 // P + H2 // P)
                step += 1
                o = bank_of(step, 1)
                for k in range(H2 // P):
                    last = nc.tensor.matmul(o, wt3_sb[:, k:k + 1], h2[:, k, cols], start=k == 0,
                                            stop=k == H2 // P - 1)
                last.then_inc(tower_done, 1)


def kernel(**inputs):
    import numpy as np
    import concourse.bacc as bacc
    from concourse.bass_utils import run_bass_kernel_spmd

    own = np.arange(F)
    w0 = np.asarray(inputs["L0_rec_filter_0"])[0]
    shift = 1 + np.arange(4 * CHUNKS)
    other = (own[None, :] + shift[:, None]) % F

    def chunked(rows):
        return np.ascontiguousarray(w0[rows.ravel()].reshape(CHUNKS, P, N).transpose(1, 0, 2))

    arrays = {
        "dense_t": np.ascontiguousarray(np.asarray(inputs["dense_ctx"]).T),
        "ids": np.ascontiguousarray(inputs["ids"]),
        "w0_pairs": chunked(own[None, :] * F + other),
        "w0_swapped": chunked(other * F + own[None, :]),
        "w0_last": np.ascontiguousarray(w0[own * F + own]),
        "w1": np.ascontiguousarray(np.asarray(inputs["L0_rec_filter_1"])[0]),
        "wt1": np.ascontiguousarray(inputs["W_top1"]), "bt1": np.ascontiguousarray(inputs["b_top1"]),
        "wt2": np.ascontiguousarray(inputs["W_top2"]), "bt2": np.ascontiguousarray(inputs["b_top2"]),
        "wt3": np.ascontiguousarray(inputs["W_top3"]),
    }
    tables = {f"tbl_{f}": np.ascontiguousarray(inputs[f"tbl_{f}"]) for f in range(F)}
    nc = bacc.Bacc("TRN2", target_bir_lowering=False, num_devices=1)

    def declare(name, a):
        return nc.dram_tensor(f"in_{name}", a.shape, mybir.dt.from_np(a.dtype), kind="ExternalInput").ap()

    args = {name: declare(name, a) for name, a in arrays.items()}
    args["tables"] = [declare(name, a) for name, a in tables.items()]
    args["out"] = nc.dram_tensor("out_y", (B, 1), F32, kind="ExternalOutput").ap()
    build_cin_tower(nc, **args)
    fed = {f"in_{name}": a for name, a in {**arrays, **tables}.items()}
    r = run_bass_kernel_spmd(nc, [fed], core_ids=[0])
    return r.results[0]["out_y"]
```
